# Optimizing a Trainium2 kernel written in Bass

```python
import numpy as np
import jax
import jax.numpy as jnp

def _softmax(x, axis=-1):
    return jax.nn.softmax(x, axis=axis)

def _gelu(x):
    return jax.nn.gelu(x, approximate=True)

def _silu(x):
    return jax.nn.silu(x)

def _sigmoid(x):
    return jax.nn.sigmoid(x)

def _layernorm(x, axis=-1, eps=1e-05):
    m = jnp.mean(x, axis=axis, keepdims=True)
    v = jnp.var(x, axis=axis, keepdims=True)
    return (x - m) / jnp.sqrt(v + eps)

def _scatter_add(tgt, idx, src, axis=0):
    return tgt.at[idx].add(src)

def _segment_sum(src, seg, n):
    return jax.ops.segment_sum(src, seg, n)
kernel_name = 'mk_gnn_preln_d1_gnn_r8_2806d4'

def setup_inputs(seed: int=0):
    np.random.seed(seed)
    _w = jnp.asarray

    def _rec_inputs():
        import jax
        import jax.numpy as jnp
        _gk = jax.random.key(seed)
        x = -0.000202 + 1 * jax.random.normal(jax.random.fold_in(_gk, 1), (12500, 64), jnp.float32)
        src = jax.random.randint(jax.random.fold_in(_gk, 2), (400000,), 0, 12500, jnp.int32)
        dst = jax.random.randint(jax.random.fold_in(_gk, 3), (400000,), 0, 12500, jnp.int32)
        _o = jnp.argsort(dst, stable=True)
        src = src[_o]
        dst = dst[_o]
        return (x, src, dst)
    x, src, dst = _rec_inputs()

    def _L0_gnn_setup():
        import jax, jax.numpy as jnp
        import numpy as np
        N_NODES = 12500
        N_EDGES = 200000
        IN_CH = 64
        OUT_CH = 64
        key = jax.random.key(seed)
        k1, k2, k3, k4 = jax.random.split(key, 4)
        x = jax.random.normal(k1, (N_NODES, IN_CH), dtype=jnp.float32)
        edge_index = jax.random.randint(k2, (2, N_EDGES), 0, N_NODES, dtype=jnp.int64)
        W1 = jax.random.normal(k3, (2 * IN_CH, OUT_CH), dtype=jnp.float32) * (1.0 / np.sqrt(2 * IN_CH))
        b1 = jnp.zeros((OUT_CH,), dtype=jnp.float32)
        W2 = jax.random.normal(k4, (OUT_CH, OUT_CH), dtype=jnp.float32) * (1.0 / np.sqrt(OUT_CH))
        b2 = jnp.zeros((OUT_CH,), dtype=jnp.float32)
        return {'x': x, 'edge_index': edge_index, 'W1': W1, 'b1': b1, 'W2': W2, 'b2': b2}
    _L0_gnn_all = _L0_gnn_setup()
    _L0_gnn_in = {k: v for k, v in _L0_gnn_all.items() if k in ('W1', 'b1', 'W2', 'b2')}
    del _L0_gnn_all
    return {'x': x, 'src': src, 'dst': dst, 'L0_gnn_W1': _L0_gnn_in['W1'], 'L0_gnn_b1': _L0_gnn_in['b1'], 'L0_gnn_W2': _L0_gnn_in['W2'], 'L0_gnn_b2': _L0_gnn_in['b2']}

def reference(x, src, dst, L0_gnn_W1, L0_gnn_b1, L0_gnn_W2, L0_gnn_b2):
    import jax
    import jax.numpy as jnp

    def _L0_gnn_ref(x, edge_index, W1, b1, W2, b2):
        import jax, jax.numpy as jnp
        import numpy as np
        N_NODES = 12500
        N_EDGES = 200000
        IN_CH = 64
        OUT_CH = 64
        src = edge_index[0]
        dst = edge_index[1]
        x_i = x[dst]
        x_j = x[src]
        feat = jnp.concatenate([x_i, x_j - x_i], axis=-1)
        h = jnp.maximum(feat @ W1 + b1, 0.0) @ W2 + b2
        out = jax.ops.segment_max(h, dst, num_segments=x.shape[0])
        return jnp.where(jnp.isneginf(out), 0.0, out)
    edge_index = jnp.stack([src, dst])
    h = jnp.maximum(_layernorm(x, axis=-1), 0.0)
    x = x + _L0_gnn_ref(h, edge_index, L0_gnn_W1, L0_gnn_b1, L0_gnn_W2, L0_gnn_b2)
    return x

_drawn_inputs = setup_inputs


def setup_inputs(seed=0):
    import zlib

    import numpy as np

    out = dict(_drawn_inputs(seed))
    spreads = {'L0_gnn_b1': (0.0, 0.1), 'L0_gnn_b2': (0.0, 0.1)}
    factors = {}
    for name, (base, spread) in spreads.items():
        noise = np.random.default_rng([zlib.crc32(name.encode()), seed]).standard_normal(out[name].shape)
        drawn = base * np.exp(spread * noise) if base else spread * noise
        out[name] = jnp.asarray(drawn.astype(out[name].dtype))
    for name, factor in factors.items():
        out[name] = (out[name] * factor).astype(out[name].dtype)
    return out
```

```python
from contextlib import ExitStack

import concourse.bass as bass
from concourse import mybir

F32 = mybir.dt.float32
BF16 = mybir.dt.bfloat16
I32 = mybir.dt.int32
U32 = mybir.dt.uint32
ALU = mybir.AluOpType
ACT = mybir.ActivationFunctionType
AX_X = mybir.AxisListType.X

FLT_MAX = 3.4028234663852886e38
EPS = 1e-5
P = 128


def edge_conv(nc, x, src, dst, W1, b1, W2, b2, out):
    N, C = x.shape
    E = src.shape[0]
    TILES = E // P
    CHUNK = 24
    RING = 10
    ITERS = TILES // (CHUNK * RING)
    CHUNKS = ITERS * RING
    TAIL = TILES - CHUNKS * CHUNK
    assert E == P * TILES and 0 < TAIL <= 8 and TAIL % 2 == 1
    W = CHUNK * C
    GROUP = 8
    GROUPS = CHUNK // GROUP
    NP = 125
    NJ = N // NP
    assert NP * NJ == N
    PIECES, PJ = 5, NJ // 5
    BLOCK = 640
    SAMPLES = E // BLOCK
    BLK_RING = 8
    BATCH = 10
    SEARCHES = NJ + 1
    BATCHES = [(a, min(a + BATCH, SEARCHES)) for a in range(0, SEARCHES, BATCH)]
    AE_RING = 5
    EARLY = 8
    ZW = 2500
    ZERO_DMAS = 8
    OUT_OF_RANGE = float(1 << 22)
    GATHER = 16 * CHUNK

    with ExitStack() as ctx:
        def sb(name, shape, dt=F32):
            return ctx.enter_context(nc.sbuf_tensor(name, shape, dt))

        def psum(name, shape, dt=F32):
            return ctx.enter_context(nc.psum_tensor(name, shape, dt))

        def sem(name):
            return ctx.enter_context(nc.semaphore(name))

        a_table = nc.dram_tensor("a_table", [N, C], F32).ap()
        b_table = nc.dram_tensor("b_table", [N, C], F32).ap()
        a_edges = nc.dram_tensor("a_edges", [E, C], F32).ap()
        states = nc.dram_tensor("states", [E, C], F32).ap()

        rows = sb("rows", [P, RING, W])
        a_fill = sb("a_fill", [P, AE_RING, W])
        state = sb("state", [P, 2, W])
        zt = sb("zt", [P, GROUPS, 512])
        src_idx = sb("src_idx", [P, RING, CHUNK], I32)
        same = sb("same", [P, TILES + CHUNK])
        keep = sb("keep", [P, 2, 2, CHUNK])
        dst_all = sb("dst_all", [P, TILES + 1], I32)
        xs = sb("xs", [P, NJ, C])
        a_rows = sb("a_rows", [P, NJ, C])
        squares = rows[:, RING - 2, 0:PJ * C]
        smp = rows[:, RING - 1, 0:SAMPLES]
        smp_f = rows[0:1, RING - 1, BLOCK:BLOCK + SAMPLES]
        ht = sb("ht", [P, 2, 256])
        blocks = a_fill[:, :, :].rearrange("p s w -> p (s w)").bitcast(I32)[:, 0:BLK_RING * BLOCK].rearrange(
            "p (s k) -> p s k", k=BLOCK)
        junk_act = zt[:, :, :].rearrange("p g w -> p (g w)").bitcast(mybir.dt.int8)
        junk_dve = sb("junk_dve", [P, 2, BLOCK], mybir.dt.int8)
        ones_row = sb("ones_row", [P, BLOCK], BF16)
        ident = sb("ident", [P, P])
        ones = sb("ones", [P, P])
        w1_raw = sb("w1_raw", [P, 2, C])
        w1_diag = sb("w1_diag", [P, 2, 2, C])
        w2_diag = sb("w2_diag", [P, 2, C])
        b1_rows = sb("b1_rows", [P, C])
        b2_rows = sb("b2_rows", [P, C])
        smp_i = sb("smp_i", [1, SAMPLES], I32)
        nid_i = sb("nid_i", [P, SEARCHES], I32)
        nid = sb("nid", [P, SEARCHES])
        nid_half = sb("nid_half", [P, SEARCHES])
        sign1 = sb("sign1", [P, SEARCHES])
        blk2 = sb("blk2", [P, SEARCHES])
        blk_idx = sb("blk_idx", [P, SEARCHES], I32)
        below = sb("below", [P, SEARCHES])
        first = sb("first", [P, SEARCHES])
        empty = sb("empty", [P, NJ])
        first_idx = sb("first_idx", [P, NJ], I32)
        last_idx = sb("last_idx", [P, NJ], I32)
        tmp_n = sb("tmp_n", [P, NJ])
        stat = sb("stat", [P, PIECES, 5, PJ])
        eps = sb("eps", [P, 1])
        lane = sb("lane", [P, 12])
        lane_i = sb("lane_i", [P, 2], I32)
        diag = sb("diag", [P, 2, P])
        caps = sb("caps", [C, 2, P])
        carry = sb("carry", [C, P])
        carry_cap = sb("carry_cap", [C, P])
        head = sb("head", [P, C])
        head_new = sb("head_new", [P, C])

        ps_t = psum("ps_t", [P, GROUPS, 512])
        ps_m = psum("ps_m", [P, GROUPS, 512])
        ps_s = psum("ps_s", [P, 2, 512])

        x_loaded = [sem(f"x_loaded{q}") for q in range(PIECES)]
        weights_loaded = sem("weights_loaded")
        w2_loaded = sem("w2_loaded")
        samples_loaded = sem("samples_loaded")
        dst_loaded = sem("dst_loaded")
        zero_row_set = sem("zero_row_set")
        zeros_stored = sem("zeros_stored")
        w2_cleared = sem("w2_cleared")
        pool_const = sem("pool_const")
        pool_step = sem("pool_step")
        dve_step = sem("dve_step")
        fill_step = sem("fill_step")
        max_step = sem("max_step")
        samples_f = sem("samples_f")
        samples_bc = sem("samples_bc")
        samples_sb = sem("samples_sb")
        consts_set = sem("consts_set")
        level1_done = sem("level1_done")
        blk_ready = sem("blk_ready")
        blk_loaded = [sem(f"blk_loaded{s}") for s in range(BLK_RING)]
        blk_used = sem("blk_used")
        centred = sem("centred")
        squared = sem("squared")
        var_ready = sem("var_ready")
        sd_ready = sem("sd_ready")
        h_ready = sem("h_ready")
        ht_ps = sem("ht_ps")
        ht_ready = sem("ht_ready")
        ab_ps = sem("ab_ps")
        a_ready = sem("a_ready")
        b_ready = sem("b_ready")
        w1_ready = sem("w1_ready")
        b_stored = sem("b_stored")
        a_stored = sem("a_stored")
        scatter_ready = sem("scatter_ready")
        a_scattered = sem("a_scattered")
        lane_idx_ready = sem("lane_idx_ready")
        first_count = sem("first_count")
        fill_init = sem("fill_init")
        diag_ready = sem("diag_ready")
        caps_ps = sem("caps_ps")
        caps_ready = sem("caps_ready")
        same_ready = sem("same_ready")
        src_first = sem("src_first")
        chunk_open = sem("chunk_open")
        src_loaded = [sem(f"src_loaded{s}") for s in range(RING)]
        gathered = [sem(f"gathered{s}") for s in range(RING)]
        a_loaded = [sem(f"a_loaded{s}") for s in range(AE_RING)]
        a_free = sem("a_free")
        keep_ready = sem("keep_ready")
        z_ready = sem("z_ready")
        z_turned = sem("z_turned")
        relu_done = sem("relu_done")
        messages = sem("messages")
        state_ready = sem("state_ready")
        state_stored = [sem(f"state_stored{s}") for s in range(2)]
        last_turned = sem("last_turned")
        carry_ready = sem("carry_ready")
        carry_turned = sem("carry_turned")
        head_loaded = sem("head_loaded")
        head_ready = sem("head_ready")
        head_stored = sem("head_stored")
        maxima_preset = sem("maxima_preset")
        maxima = [sem(f"maxima{g}") for g in range(NJ // BATCH)]
        x_again = sem("x_again")
        out_ready = sem("out_ready")
        out_stored = sem("out_stored")

        x_nodes = x.rearrange("(p j) c -> p j c", p=NP)
        out_nodes = out.rearrange("(p j) c -> p j c", p=NP)
        a_nodes = a_table.rearrange("(p j) c -> p j c", p=NP)
        b_nodes = b_table.rearrange("(p j) c -> p j c", p=NP)
        src_lanes = src.rearrange("(p t) -> p t", p=P)
        dst_lanes = dst.rearrange("(p t) -> p t", p=P)
        dst_blocks = dst.rearrange("(b k) -> b k", k=BLOCK)
        a_lanes = a_edges.rearrange("(p t) c -> p (t c)", p=P)
        state_lanes = states.rearrange("(p t) c -> p (t c)", p=P)

        def at(index, column):
            return bass.IndirectOffsetOnAxis(ap=index[:, column:column + 1], axis=0)

        def pairs(tiles):
            return [(k, min(2, tiles - k)) for k in range(0, tiles, 2)]

        def groups(tiles):
            return [(g, min(GROUP, tiles - g * GROUP)) for g in range((tiles + GROUP - 1) // GROUP)]

        block = ctx.enter_context(nc.Block())

        @block.sync
        def _(sp):
            for q in range(PIECES):
                sp.dma_start(xs[0:NP, q * PJ:(q + 1) * PJ, :],
                             x_nodes[:, q * PJ:(q + 1) * PJ, :]).then_inc(x_loaded[q], 16)
            sp.dma_start(dst_all[:, 1:], dst_lanes).then_inc(dst_loaded, 16)
            sp.dma_start(src_idx[:, :, :].rearrange("p r k -> p (r k)"),
                         src_lanes[:, 0:RING * CHUNK]).then_inc(src_first, 16)
            sp.dma_start(b1_rows[0:NP, :], b1.rearrange("(o c) -> o c", o=1).to_broadcast((NP, C))
                         ).then_inc(weights_loaded, 16)
            sp.dma_start(b2_rows[0:NP, :], b2.rearrange("(o c) -> o c", o=1).to_broadcast((NP, C))
                         ).then_inc(weights_loaded, 16)
            sp.wait_ge(w2_cleared, 1)
            for h in range(2):
                sp.dma_start(w2_diag[h * C:(h + 1) * C, h, :], W2).then_inc(w2_loaded, 16)
            sp.wait_ge(zero_row_set, 1)
            reps = TILES * C // ZW
            for z in range(ZERO_DMAS):
                n = reps // ZERO_DMAS
                dst_ap = a_lanes[:, z * n * ZW:(z + 1) * n * ZW].rearrange("p (r w) -> p r w", w=ZW)
                zero = state[:, :, :].rearrange("p s w -> p (s w)")[:, 0:ZW].rearrange("p (o w) -> p o w", o=1)
                sp.dma_start(dst_ap, zero.to_broadcast((P, n, ZW))).then_inc(zeros_stored, 16)
                if z < PIECES:
                    sp.wait_ge(b_ready, (z + 1) * PJ // 4)
                    sp.dma_start(b_nodes[:, z * PJ:(z + 1) * PJ, :],
                                 xs[0:NP, z * PJ:(z + 1) * PJ, :]).then_inc(b_stored, 16)
                    sp.wait_ge(a_ready, (z + 1) * PJ // 4)
                    sp.dma_start(a_nodes[:, z * PJ:(z + 1) * PJ, :],
                                 a_rows[0:NP, z * PJ:(z + 1) * PJ, :]).then_inc(a_stored, 16)
            sp.wait_ge(b_stored, 16 * PIECES)
            sp.dma_start(xs[0:NP, :, :], x_nodes).then_inc(x_again, 16)
            sp.wait_ge(zeros_stored, 16 * ZERO_DMAS)
            sp.wait_ge(a_scattered, 16 * NJ)

            def load_a(c, k, tiles=CHUNK):
                sp.wait_ge(a_free, c + 1)
                sp.dma_start(a_fill[:, k % AE_RING, 0:tiles * C],
                             a_lanes[:, bass.ds(c * W, tiles * C)]).then_inc(a_loaded[k % AE_RING], 16)

            with sp.Fori(0, ITERS - 1) as i:
                for k in range(RING):
                    load_a(i * RING + k, k)
                    sp.wait_ge(gathered[k], (i + 1) * GATHER)
                    sp.dma_start(src_idx[:, k, :], src_lanes[:, bass.ds((i * RING + RING + k) * CHUNK, CHUNK)]
                                 ).then_inc(src_loaded[k], 16)
            for k in range(RING):
                load_a((ITERS - 1) * RING + k, k)
                if k == 0:
                    sp.wait_ge(gathered[0], ITERS * GATHER)
                    sp.dma_start(src_idx[:, 0, 0:TAIL], src_lanes[:, CHUNKS * CHUNK:TILES]
                                 ).then_inc(src_loaded[0], 16)
            load_a(CHUNKS, RING, TAIL)
            for g in range(NJ // BATCH):
                sp.wait_ge(out_ready, g + 1)
                sp.dma_start(out_nodes[:, g * BATCH:(g + 1) * BATCH, :],
                             a_rows[0:NP, g * BATCH:(g + 1) * BATCH, :]).then_inc(out_stored, 16)
            sp.wait_ge(out_stored, 16 * (NJ // BATCH))

        @block.gpsimd
        def _(pool):
            nc.gpsimd.iota(nid_i[0:NP, :], pattern=[[1, SEARCHES]], base=0, channel_multiplier=NJ).then_inc(pool_const, 1)
            nc.gpsimd.memset(ones[:, :], 1.0).then_inc(pool_step, 1)
            nc.gpsimd.memset(ident[:, :], 0.0).then_inc(pool_step, 1)
            nc.gpsimd.iota(lane_i[:, 0:1], pattern=[[0, 1]], base=-1, channel_multiplier=TILES).then_inc(pool_const, 1)
            pool.wait_ge(pool_step, 2)
            nc.gpsimd.affine_select(out=ident[:, :], in_=ident[:, :], compare_op=ALU.not_equal, fill=1.0, base=0,
                                    pattern=[[-1, P]], channel_multiplier=1).then_inc(pool_const, 1)

            def gather_chunk(slot, tiles=CHUNK):
                for t in range(tiles):
                    nc.gpsimd.indirect_dma_start(
                        out=rows[:, slot, t * C:(t + 1) * C], out_offset=None,
                        in_=b_table, in_offset=at(src_idx[:, slot, :], t)).then_inc(gathered[slot], 16)

            for j in range(SEARCHES):
                if j % BATCH == 0:
                    pool.wait_ge(blk_ready, j // BATCH + 1)
                if j >= BLK_RING:
                    pool.wait_ge(blk_used, j - BLK_RING + 1)
                nc.gpsimd.indirect_dma_start(
                    out=blocks[0:NP, j % BLK_RING, :], out_offset=None,
                    in_=dst_blocks, in_offset=at(blk_idx[0:NP, :], j)).then_inc(blk_loaded[j % BLK_RING], 16)
            pool.wait_ge(src_first, 16)
            pool.wait_ge(b_stored, 16 * PIECES)
            for c in range(EARLY):
                gather_chunk(c)
            pool.wait_ge(lane_idx_ready, 1)
            pool.wait_ge(a_stored, 16 * PIECES)
            pool.wait_ge(zeros_stored, 16 * ZERO_DMAS)
            nc.gpsimd.indirect_dma_start(
                out=a_fill[:, AE_RING - 1, W - C:W], out_offset=None,
                in_=a_table, in_offset=at(dst_all[:, :], 1)).then_inc(fill_init, 16)
            pool.wait_ge(scatter_ready, 1)
            for j in range(NJ):
                nc.gpsimd.indirect_dma_start(
                    out=a_edges, out_offset=at(first_idx[0:NP, :], j), in_=a_rows[0:NP, j, :], in_offset=None,
                    bounds_check=E - 1, oob_is_err=False).then_inc(a_scattered, 16)
            for c in range(EARLY, RING):
                gather_chunk(c)
            with pool.Fori(1, ITERS) as i:
                for k in range(RING):
                    pool.wait_ge(z_turned, (i * RING + k - RING + 1) * GROUPS)
                    pool.wait_ge(src_loaded[k], i * 16)
                    pool.sem_inc(chunk_open, 1)
                    gather_chunk(k)
            pool.wait_ge(z_turned, (CHUNKS - RING + 1) * GROUPS)
            pool.wait_ge(src_loaded[0], ITERS * 16)
            gather_chunk(0, TAIL)

            pool.wait_ge(state_stored[0], 16 * (CHUNKS // 2 + 2))
            pool.wait_ge(state_stored[1], 16 * (CHUNKS // 2 + 1))
            nc.gpsimd.indirect_dma_start(
                out=head[:, :], out_offset=None, in_=states, in_offset=at(lane_i, 1)).then_inc(head_loaded, 16)
            pool.wait_ge(head_ready, 1)
            nc.gpsimd.indirect_dma_start(
                out=states, out_offset=at(lane_i, 1), in_=head_new[:, :], in_offset=None).then_inc(head_stored, 16)
            pool.wait_ge(head_stored, 16)
            pool.wait_ge(maxima_preset, 1)
            for j in range(NJ):
                nc.gpsimd.indirect_dma_start(
                    out=a_rows[0:NP, j, :], out_offset=None, in_=states, in_offset=at(last_idx[0:NP, :], j),
                    bounds_check=E - 1, oob_is_err=False).then_inc(maxima[j // BATCH], 16)

        @block.scalar
        def _(act):
            act.dma_start(smp_i[:, :], dst_blocks[:, 0:1].rearrange("b o -> o b"),
                          allow_slow_non_contiguous=True).then_inc(samples_loaded, 16)
            act.dma_start(dst_all[1:P, 0:1], dst_lanes[0:P - 1, TILES - 1:TILES],
                          allow_slow_non_contiguous=True).then_inc(dst_loaded, 16)
            for h in range(2):
                act.dma_start(w1_raw[h * C:(h + 1) * C, :, :],
                              W1.rearrange("(h c) n -> c h n", h=2)).then_inc(weights_loaded, 16)

            def level1(a, b):
                for j in range(a, b):
                    if j >= 2:
                        act.wait_ge(level1_done, j - 1)
                    nc.scalar.activation(junk_act[0:NP, j % 2 * BLOCK:j % 2 * BLOCK + SAMPLES], smp[0:NP, :], ACT.Sign,
                                         scale=-1.0, bias=nid_half[0:NP, j:j + 1],
                                         accum_out=sign1[0:NP, j:j + 1]).then_inc(level1_done, 1)

            def square(q):
                act.wait_ge(centred, q + 1)
                if q >= 1:
                    act.wait_ge(var_ready, q)
                nc.scalar.activation(squares[0:NP, :], xs[0:NP, q * PJ:(q + 1) * PJ, :].rearrange("p j c -> p (j c)"),
                                     ACT.Square).then_inc(squared, 1)

            def deviation(q):
                act.wait_ge(var_ready, q + 1)
                nc.scalar.activation(stat[0:NP, q, 3, :], stat[0:NP, q, 2, :], ACT.Sqrt, scale=1.0 / C,
                                     bias=eps[0:NP, :]).then_inc(sd_ready, 1)

            def evacuate(g):
                if g < NJ // 4:
                    act.wait_ge(ht_ps, g + 1)
                    if g >= 2:
                        act.wait_ge(ab_ps, g - 1)
                    nc.scalar.activation(ht[:, g % 2, 0:2 * NP], ps_t[:, g % 2, 0:2 * NP], ACT.Relu).then_inc(ht_ready, 1)
                if g >= 1:
                    act.wait_ge(a_ready, g)
                    nc.scalar.activation(xs[0:NP, 4 * (g - 1):4 * g, :],
                                         ps_m[0:NP, (g - 1) % 2, :].rearrange("p (j w) -> p j w", j=4)[:, :, C:2 * C],
                                         ACT.Copy).then_inc(b_ready, 1)

            act.wait_ge(consts_set, 1)
            act.wait_ge(samples_sb, 1)
            for n, (a, b) in enumerate(BATCHES):
                level1(a, b)
                if n < PIECES:
                    square(n)
                if 1 <= n <= PIECES:
                    deviation(n - 1)
            for g in range(NJ // 4 + 1):
                evacuate(g)

            act.wait_ge(level1_done, SEARCHES)
            act.wait_ge(lane_idx_ready, 1)
            nc.scalar.activation(junk_act[:, 0:TILES], dst_all[:, 1:], ACT.Sign, scale=-1.0, bias=lane[:, 0:1],
                                 accum_out=lane[:, 1:2]).then_inc(first_count, 1)

            def flags(c, k, tiles=CHUNK):
                now = same[:, bass.ds(c * CHUNK, CHUNK)]
                nc.scalar.activation(keep[:, k % 2, 0, :], now, ACT.Relu)
                nc.scalar.activation(keep[:, k % 2, 1, :], now, ACT.Copy, scale=FLT_MAX).then_inc(keep_ready, 1)

            def step(c, k, tiles=CHUNK):
                if tiles == CHUNK:
                    flags(c + 1, k + 1)
                for g, n in groups(tiles):
                    act.wait_ge(z_turned, c * GROUPS + g + 1)
                    full = n // 2 * P
                    last = nc.scalar.activation(zt[:, g, 0:full], ps_t[:, g, 0:full], ACT.Relu)
                    if n % 2:
                        last = nc.scalar.activation(zt[0:C, g, full:full + P], ps_t[0:C, g, full:full + P], ACT.Relu)
                    last.then_inc(relu_done, 1)
                act.wait_ge(state_ready, c + 1)
                act.dma_start(state_lanes[:, bass.ds(c * W, tiles * C)], state[:, k % 2, 0:tiles * C]
                              ).then_inc(state_stored[k % 2], 16)

            act.wait_ge(same_ready, 1)
            flags(0, 0)
            for half in range(2):
                act.sem_inc(state_stored[half], 16)
            with act.Fori(0, ITERS) as i:
                for k in range(RING):
                    step(i * RING + k, k)
            step(CHUNKS, 0, TAIL)
            act.wait_ge(state_stored[0], 16 * (CHUNKS // 2 + 2))
            act.wait_ge(state_stored[1], 16 * (CHUNKS // 2 + 1))

        @block.tensor
        def _(pe):
            pe.wait_ge(samples_f, 1)
            pe.wait_ge(pool_const, 3)
            for a in range(0, SAMPLES, 512):
                b = min(SAMPLES, a + 512)
                last = nc.tensor.matmul(ps_s[0:NP, a // 512, 0:b - a], ones[0:1, 0:NP], smp_f[:, a:b], start=True, stop=True)
            last.then_inc(samples_bc, 1)

            def turn_h(g):
                if 4 * g % PJ == 0:
                    pe.wait_ge(h_ready, 4 * g // PJ + 1)
                if g >= 2:
                    pe.wait_ge(ht_ready, g - 1)
                for a in range(2):
                    last = nc.tensor.transpose(ps_t[:, g % 2, a * NP:(a + 1) * NP],
                                               xs[0:NP, 4 * g + 2 * a:4 * g + 2 * a + 2, :].rearrange("p j c -> p (j c)"),
                                               ident[0:NP, 0:NP])
                last.then_inc(ht_ps, 1)

            def products(g):
                pe.wait_ge(ht_ready, g + 1)
                if g >= 2:
                    pe.wait_ge(a_ready, g - 1)
                    pe.wait_ge(b_ready, g - 1)
                for a in range(2):
                    last = nc.tensor.matmul(ps_m[0:NP, g % 2, a * 2 * P:(a + 1) * 2 * P], ht[:, g % 2, a * NP:(a + 1) * NP],
                                            w1_diag[:, :, :, :].rearrange("p h w n -> p (h w n)"), start=True, stop=True)
                last.then_inc(ab_ps, 1)

            pe.wait_ge(w1_ready, 4)
            for g in range(NJ // 4 + 1):
                if g < NJ // 4:
                    turn_h(g)
                if g >= 1:
                    products(g - 1)

            pe.wait_ge(diag_ready, 1)
            for f in range(2):
                last = nc.tensor.matmul(ps_s[0:C, 0, f * P:(f + 1) * P], ones[:, 0:C], diag[:, f, :], start=True, stop=True)
            last.then_inc(caps_ps, 1)
            pe.wait_ge(w2_loaded, 32)
            pe.wait_ge(a_ready, NJ // 4)
            pe.wait_ge(b_ready, NJ // 4)

            w2_pair = w2_diag[:, :, :].rearrange("p h n -> p (h n)")

            def step(c, slot, tiles=CHUNK):
                pe.wait_ge(z_ready, c + 1)
                for g, n in groups(tiles):
                    for k, m in pairs(n):
                        t = g * GROUP + k
                        last = nc.tensor.transpose(ps_t[0:m * C, g, k * C:k * C + P],
                                                   rows[:, slot, t * C:(t + m) * C], ident[:, :])
                    last.then_inc(z_turned, 1)
                for g, n in groups(tiles):
                    pe.wait_ge(relu_done, c * GROUPS + g + 1)
                    for k, m in pairs(n):
                        last = nc.tensor.matmul(ps_m[:, g, k * C:(k + m) * C], zt[0:m * C, g, k * C:k * C + P],
                                                w2_pair[0:m * C, 0:m * C], start=True, stop=True)
                    last.then_inc(messages, 1)

            with pe.Fori(0, ITERS) as i:
                for k in range(RING):
                    step(i * RING + k, k)
            step(CHUNKS, 0, TAIL)

            pe.wait_ge(state_ready, CHUNKS + 1)
            pe.wait_ge(caps_ready, 1)
            nc.tensor.transpose(ps_s[0:C, 0, 0:P], state[:, 0, (TAIL - 1) * C:TAIL * C], ident[:, :]).then_inc(last_turned, 1)
            pe.wait_ge(carry_ready, 1)
            nc.tensor.transpose(ps_s[:, 1, 0:C], carry_cap[:, :], ident[0:C, 0:C]).then_inc(carry_turned, 1)

        @block.vector
        def _(dve):
            steps = [0]

            def link(instruction):
                steps[0] += 1
                instruction.then_inc(dve_step, 1)
                dve.wait_ge(dve_step, steps[0])

            nc.vector.memset(w2_diag[:, :, :], 0.0).then_inc(w2_cleared, 1)
            nc.vector.memset(state[:, :, :], 0.0).then_inc(zero_row_set, 1)
            nc.vector.memset(eps[:, :], EPS)
            link(nc.vector.memset(w1_diag[:, :, :, :], 0.0))
            nc.vector.memset(ones_row[:, :], 1.0)
            nc.vector.memset(same[:, TILES:], 0.0)
            nc.vector.memset(dst_all[0:1, 0:1], -1)
            dve.wait_ge(pool_const, 3)
            link(nc.vector.tensor_copy(nid[0:NP, :], nid_i[0:NP, :]))
            nc.vector.tensor_scalar(nid_half[0:NP, :], nid[0:NP, :], -0.5, None, ALU.add).then_inc(consts_set, 1)
            dve.wait_ge(samples_loaded, 16)
            nc.vector.tensor_copy(smp_f[:, :], smp_i[:, :]).then_inc(samples_f, 1)
            dve.wait_ge(samples_bc, 1)
            nc.vector.tensor_copy(smp[0:NP, :], ps_s[0:NP, :, :].rearrange("p s w -> p (s w)")[:, 0:SAMPLES]).then_inc(samples_sb, 1)
            dve.wait_ge(weights_loaded, 64)
            for h in range(2):
                half = slice(h * C, (h + 1) * C)
                nc.vector.tensor_tensor(w1_diag[half, h, 0, :], w1_raw[half, 0, :], w1_raw[half, 1, :],
                                        ALU.subtract).then_inc(w1_ready, 1)
                nc.vector.tensor_copy(w1_diag[half, h, 1, :], w1_raw[half, 1, :]).then_inc(w1_ready, 1)

            def block_indices(n):
                a, b = BATCHES[n]
                dve.wait_ge(level1_done, b)
                link(nc.vector.tensor_scalar(blk2[0:NP, a:b], sign1[0:NP, a:b], float(SAMPLES - 2), 0.0, ALU.add, ALU.max))
                nc.vector.tensor_scalar(blk_idx[0:NP, a:b], blk2[0:NP, a:b], 0.5, None, ALU.mult).then_inc(blk_ready, 1)

            def piece(q):
                return xs[0:NP, q * PJ:(q + 1) * PJ, :]

            def spread(values):
                return values.rearrange("p (j o) -> p j o", o=1).to_broadcast((NP, PJ, C))

            def centre(q):
                dve.wait_ge(x_loaded[q], 16)
                s = stat[0:NP, q, :, :]
                link(nc.vector.tensor_reduce(s[:, 0, :], piece(q), AX_X, ALU.add))
                link(nc.vector.tensor_scalar(s[:, 1, :], s[:, 0, :], 1.0 / C, None, ALU.mult))
                nc.vector.tensor_tensor(piece(q), piece(q), spread(s[:, 1, :]), ALU.subtract).then_inc(centred, 1)

            def scale(q):
                s = stat[0:NP, q, :, :]
                dve.wait_ge(squared, q + 1)
                nc.vector.tensor_reduce(s[:, 2, :], squares[0:NP, :].rearrange("p (j c) -> p j c", c=C),
                                        AX_X, ALU.add).then_inc(var_ready, 1)
                dve.wait_ge(sd_ready, q + 1)
                link(nc.vector.reciprocal(s[:, 4, :], s[:, 3, :]))
                nc.vector.tensor_tensor(piece(q), piece(q), spread(s[:, 4, :]), ALU.mult).then_inc(h_ready, 1)

            for q in range(PIECES + 1):
                if q < PIECES:
                    block_indices(q)
                    centre(q)
                if q >= 1:
                    scale(q - 1)
            for n in range(PIECES, len(BATCHES)):
                block_indices(n)

            def count_block(j):
                dve.wait_ge(blk_loaded[j % BLK_RING], 16 * (j // BLK_RING + 1))
                if j >= 2:
                    dve.wait_ge(blk_used, j - 1)
                nc.vector.scalar_tensor_tensor(junk_dve[0:NP, j % 2, :], blocks[0:NP, j % BLK_RING, :], nid[0:NP, j:j + 1],
                                               ones_row[0:NP, :], ALU.is_lt, ALU.mult,
                                               accum_out=below[0:NP, j:j + 1]).then_inc(blk_used, 1)

            for g in range(NJ // 4):
                dve.wait_ge(ab_ps, g + 1)
                nc.vector.tensor_tensor(a_rows[0:NP, 4 * g:4 * g + 4, :],
                                        ps_m[0:NP, g % 2, :].rearrange("p (j w) -> p j w", j=4)[:, :, 0:C],
                                        b1_rows[0:NP, :].rearrange("p (o c) -> p o c", o=1).to_broadcast((NP, 4, C)),
                                        ALU.add).then_inc(a_ready, 1)
                for j in range(2 * g, 2 * g + 2):
                    count_block(j)
            for j in range(NJ // 2, SEARCHES):
                count_block(j)
            dve.wait_ge(blk_used, SEARCHES)
            link(nc.vector.scalar_tensor_tensor(first[0:NP, :], blk2[0:NP, :], BLOCK / 2.0, below[0:NP, :], ALU.mult, ALU.add))
            link(nc.vector.tensor_tensor(empty[0:NP, :], first[0:NP, 0:NJ], first[0:NP, 1:SEARCHES], ALU.is_equal))
            nc.vector.scalar_tensor_tensor(first_idx[0:NP, :], empty[0:NP, :], OUT_OF_RANGE, first[0:NP, 0:NJ],
                                           ALU.mult, ALU.add).then_inc(scatter_ready, 1)
            link(nc.vector.tensor_scalar(tmp_n[0:NP, :], first[0:NP, 1:SEARCHES], -1.0, 0.0, ALU.add, ALU.max))
            nc.vector.scalar_tensor_tensor(last_idx[0:NP, :], empty[0:NP, :], OUT_OF_RANGE, tmp_n[0:NP, :],
                                           ALU.mult, ALU.add)

            dve.wait_ge(dst_loaded, 32)
            nc.vector.tensor_scalar(lane[:, 0:1], dst_all[:, 1:2], 0.5, None, ALU.add).then_inc(lane_idx_ready, 1)
            link(nc.vector.tensor_tensor(same[:, 0:TILES], dst_all[:, 1:], dst_all[:, 0:TILES], ALU.is_equal))
            link(nc.vector.tensor_tensor(lane[:, 2:3], dst_all[:, 1:2], dst_all[:, TILES:TILES + 1], ALU.is_equal))
            link(nc.vector.tensor_tensor(lane[:, 3:4], lane[:, 2:3], same[:, 0:1], ALU.mult))
            dve.wait_ge(pool_const, 3)
            nc.vector.tensor_scalar(diag[:, 0, :], ident[:, :], same[:, 0:1], None, ALU.mult)
            nc.vector.tensor_scalar(diag[:, 1, :], ident[:, :], lane[:, 3:4], None, ALU.mult).then_inc(diag_ready, 1)
            dve.wait_ge(diag_ready, 1)
            nc.vector.tensor_scalar(same[:, 0:TILES], same[:, 0:TILES], 2.0, -1.0, ALU.mult, ALU.add).then_inc(same_ready, 1)
            dve.wait_ge(caps_ps, 1)
            link(nc.vector.tensor_scalar(caps[:, :, :].rearrange("p f q -> p (f q)"), ps_s[0:C, 0, 0:2 * P],
                                         2.0, -1.0, ALU.mult, ALU.add))
            link(nc.vector.tensor_scalar(caps[:, :, :], caps[:, :, :], FLT_MAX, None, ALU.mult))
            dve.wait_ge(first_count, 1)
            link(nc.vector.tensor_scalar(lane[:, 4:5], lane[:, 1:2], float(TILES), 0.5, ALU.add, ALU.mult))
            link(nc.vector.tensor_copy(lane[:, 5:6], lane_i[:, 0:1]))
            nc.vector.tensor_tensor(lane_i[:, 1:2], lane[:, 4:5], lane[:, 5:6], ALU.add).then_inc(caps_ready, 1)

            dve.wait_ge(zeros_stored, 16 * ZERO_DMAS)
            nc.vector.memset(state[:, 1, W - C:W], -FLT_MAX).then_inc(a_free, AE_RING - 1)
            dve.wait_ge(a_scattered, 16 * NJ)
            nc.vector.tensor_scalar(a_rows[0:NP, :, :], b2_rows[0:NP, :].rearrange("p (o c) -> p o c", o=1)
                                    .to_broadcast((NP, NJ, C)), -1.0, None, ALU.mult).then_inc(maxima_preset, 1)
            dve.wait_ge(fill_init, 16)
            dve.wait_ge(a_free, AE_RING - 1)

            def step(c, k, i, tiles=CHUNK):
                slot, half = k % AE_RING, k % 2
                fill_before, max_before = c * CHUNK, c * CHUNK
                dve.wait_ge(a_loaded[slot], (i * 2 + k // AE_RING + 1) * 16)
                dve.wait_ge(keep_ready, c + 1)
                for t in range(tiles):
                    if t == 0:
                        before = a_fill[:, (slot - 1) % AE_RING, W - C:W]
                    else:
                        before = a_fill[:, slot, (t - 1) * C:t * C]
                        dve.wait_ge(fill_step, fill_before + t)
                    here = a_fill[:, slot, t * C:(t + 1) * C]
                    fill = nc.vector.scalar_tensor_tensor(here, before, keep[:, half, 0, t:t + 1], here, ALU.mult, ALU.add)
                    fill.then_inc(fill_step, 1)
                    if t == 0:
                        dve.wait_ge(fill_step, fill_before + 1)
                        dve.sem_inc(a_free, 1)
                dve.wait_ge(fill_step, fill_before + tiles)
                dve.wait_ge(gathered[k % RING], i * GATHER + 16 * tiles)
                now = rows[:, k % RING, 0:tiles * C]
                nc.vector.tensor_tensor(now, now, a_fill[:, slot, 0:tiles * C], ALU.add).then_inc(z_ready, 1)
                dve.wait_ge(state_stored[half], (i * (RING // 2) + k // 2 + 1) * 16)
                for t in range(tiles):
                    g, r = divmod(t, GROUP)
                    if r == 0:
                        dve.wait_ge(messages, c * GROUPS + g + 1)
                    if t == 0:
                        before = state[:, 1 - half, W - C:W]
                    else:
                        before = state[:, half, (t - 1) * C:t * C]
                        dve.wait_ge(max_step, max_before + t)
                    best = nc.vector.scalar_tensor_tensor(state[:, half, t * C:(t + 1) * C], before,
                                                          keep[:, half, 1, t:t + 1], ps_m[:, g, r * C:(r + 1) * C],
                                                          ALU.min, ALU.max)
                    best.then_inc(max_step, 1)
                dve.wait_ge(max_step, max_before + tiles)
                dve.sem_inc(state_ready, 1)

            with dve.Fori(0, ITERS) as i:
                for k in range(RING):
                    step(i * RING + k, k, i)
            step(CHUNKS, 0, ITERS, TAIL)

            dve.wait_ge(last_turned, 1)
            nc.vector.memset(carry[:, 0:1], -FLT_MAX)
            link(nc.vector.tensor_tensor_scan(carry[:, 1:P], caps[:, 1, 0:P - 1], ps_s[0:C, 0, 0:P - 1], -FLT_MAX,
                                              ALU.min, ALU.max))
            nc.vector.tensor_tensor(carry_cap[:, :], carry[:, :], caps[:, 0, :], ALU.min).then_inc(carry_ready, 1)
            dve.wait_ge(carry_turned, 1)
            dve.wait_ge(head_loaded, 16)
            nc.vector.tensor_tensor(head_new[:, :], head[:, :], ps_s[:, 1, 0:C], ALU.max).then_inc(head_ready, 1)

            dve.wait_ge(x_again, 16)
            for g in range(NJ // BATCH):
                dve.wait_ge(maxima[g], 16 * BATCH)
                part = a_rows[0:NP, g * BATCH:(g + 1) * BATCH, :]
                link(nc.vector.tensor_tensor(part, part, b2_rows[0:NP, :].rearrange("p (o c) -> p o c", o=1)
                                             .to_broadcast((NP, BATCH, C)), ALU.add))
                nc.vector.tensor_tensor(part, part, xs[0:NP, g * BATCH:(g + 1) * BATCH, :], ALU.add).then_inc(out_ready, 1)


_INS = ["x", "src", "dst", "L0_gnn_W1", "L0_gnn_b1", "L0_gnn_W2", "L0_gnn_b2"]


def kernel(**inputs):
    import numpy as _np
    import concourse.bacc as _bacc
    from concourse import mybir as _mybir
    from concourse.bass_utils import run_bass_kernel_spmd as _run

    nc = _bacc.Bacc("TRN2", target_bir_lowering=False, num_devices=1)
    arrays, args = {}, []
    for name in _INS:
        a = _np.ascontiguousarray(inputs[name])
        arrays[f"in_{name}_dram"] = a
        args.append(nc.dram_tensor(f"in_{name}_dram", a.shape, _mybir.dt.from_np(a.dtype), kind="ExternalInput").ap())
    shape = arrays["in_x_dram"].shape
    args.append(nc.dram_tensor("out_dram", shape, _mybir.dt.float32, kind="ExternalOutput").ap())
    edge_conv(nc, *args)
    r = _run(nc, [arrays], core_ids=[0])
    return r.results[0]["out_dram"]
```

```python
from contextlib import ExitStack

import concourse.bass as bass
from concourse import mybir

F32 = mybir.dt.float32
BF16 = mybir.dt.bfloat16
I32 = mybir.dt.int32
U32 = mybir.dt.uint32
ALU = mybir.AluOpType
ACT = mybir.ActivationFunctionType
AX_X = mybir.AxisListType.X

FLT_MAX = 3.4028234663852886e38
EPS = 1e-5
P = 128


def edge_conv(nc, x, src, dst, W1, b1, W2, b2, out):
    N, C = x.shape
    E = src.shape[0]
    TILES = E // P
    CHUNK = 12
    RING = 26
    ITERS = TILES // (CHUNK * RING)
    CHUNKS = ITERS * RING
    TAIL = TILES - CHUNKS * CHUNK
    assert E == P * TILES and 0 < TAIL <= 8 and TAIL % 2 == 1
    W = CHUNK * C
    GROUP = 8
    GROUPS = (CHUNK + GROUP - 1) // GROUP
    NP = 125
    NJ = N // NP
    assert NP * NJ == N
    PIECES, PJ = 5, NJ // 5
    BLOCK = 400
    SAMPLES = E // BLOCK
    SCOLS = SAMPLES // NP
    assert SCOLS * NP == SAMPLES
    BLK_RING = 24
    BATCH = 10
    SEARCHES = NJ + 1
    AE_RING = 2
    KEEP = RING // 2
    SQUARES_AT, BLOCKS_AT = RING - 15, RING - 13
    assert RING % AE_RING == 0 and RING % 2 == 0 and BLK_RING * BLOCK <= 13 * W
    ZW, ZREP = 1250, 2
    ZEROS = TILES * C // (ZW * ZREP)
    OUT_OF_RANGE = float(1 << 22)
    GATHER = 16 * CHUNK

    with ExitStack() as ctx:
        def sb(name, shape, dt=F32):
            return ctx.enter_context(nc.sbuf_tensor(name, shape, dt))

        def psum(name, shape, dt=F32):
            return ctx.enter_context(nc.psum_tensor(name, shape, dt))

        def sem(name):
            return ctx.enter_context(nc.semaphore(name))

        a_table = nc.dram_tensor("a_table", [N, C], F32).ap()
        b_table = nc.dram_tensor("b_table", [N, C], F32).ap()
        a_edges = nc.dram_tensor("a_edges", [E, C], F32).ap()
        states = nc.dram_tensor("states", [E, C], F32).ap()

        rows = sb("rows", [P, RING, W])
        a_fill = sb("a_fill", [P, AE_RING, W])
        state = sb("state", [P, 2, W])
        zt = sb("zt", [P, GROUPS, 512])
        src_idx = sb("src_idx", [P, RING, CHUNK], I32)
        same = sb("same", [P, TILES + CHUNK])
        keep = sb("keep", [P, KEEP, 2, CHUNK])
        dst_all = sb("dst_all", [P, TILES + 1], I32)
        xs = sb("xs", [P, NJ, C])
        a_rows = sb("a_rows", [P, NJ, C])
        squares = rows[:, SQUARES_AT:SQUARES_AT + 2, :].rearrange("p s w -> p (s w)")[:, 0:PJ * C]
        ht = sb("ht", [P, 2, 256])
        blocks = rows[:, BLOCKS_AT:, :].rearrange("p s w -> p (s w)").bitcast(I32)[:, 0:BLK_RING * BLOCK].rearrange(
            "p (s k) -> p s k", k=BLOCK)
        junk_act = zt[:, :, :].rearrange("p g w -> p (g w)").bitcast(mybir.dt.int8)
        ident = sb("ident", [P, P])
        ones = sb("ones", [P, P])
        w1_raw = sb("w1_raw", [P, 2, C])
        w1_diag = sb("w1_diag", [P, 2, 2, C])
        w2_diag = sb("w2_diag", [P, 2, C])
        b1_rows = sb("b1_rows", [P, C])
        b2_rows = sb("b2_rows", [P, C])
        smp_i = sb("smp_i", [P, SCOLS], I32)
        smp = sb("smp", [P, 4, SCOLS])
        rank_i = sb("rank_i", [P, P + 1], I32)
        rank = sb("rank", [P, P + 1])
        base = sb("base", [P, P])
        above = sb("above", [P, SCOLS, P], BF16)
        inside = sb("inside", [P, SCOLS, P], BF16)
        column = sb("column", [P, SCOLS, SEARCHES], BF16)
        ones_b = sb("ones_b", [P, SEARCHES], BF16)
        nid_i = sb("nid_i", [P, SEARCHES], I32)
        nid_half = sb("nid_half", [P, SEARCHES])
        blk = sb("blk", [P, SEARCHES])
        blk_idx = sb("blk_idx", [P, SEARCHES], I32)
        below = sb("below", [P, SEARCHES])
        first = sb("first", [P, SEARCHES])
        empty = sb("empty", [P, NJ])
        first_idx = sb("first_idx", [P, NJ], I32)
        last_idx = sb("last_idx", [P, NJ], I32)
        tmp_n = sb("tmp_n", [P, NJ])
        stat = sb("stat", [P, PIECES, 5, PJ])
        eps = sb("eps", [P, 1])
        lane = sb("lane", [P, 12])
        lane_i = sb("lane_i", [P, 2], I32)
        diag = sb("diag", [P, 2, P])
        caps = sb("caps", [C, 2, P])
        carry = sb("carry", [C, P])
        carry_cap = sb("carry_cap", [C, P])
        head = sb("head", [P, C])
        head_new = sb("head_new", [P, C])

        ps_t = psum("ps_t", [P, GROUPS, 512])
        ps_m = psum("ps_m", [P, GROUPS, 512])
        ps_s = psum("ps_s", [P, 2, 512])

        x_loaded = [sem(f"x_loaded{q}") for q in range(PIECES)]
        weights_loaded = sem("weights_loaded")
        w2_loaded = sem("w2_loaded")
        samples_loaded = sem("samples_loaded")
        dst_loaded = sem("dst_loaded")
        zero_row_set = sem("zero_row_set")
        zeros_stored = [sem(f"zeros_stored{s}") for s in range(2)]
        w2_cleared = sem("w2_cleared")
        pool_const = sem("pool_const")
        pool_step = sem("pool_step")
        pool_ranks = sem("pool_ranks")
        dve_step = sem("dve_step")
        fill_step = sem("fill_step")
        max_step = sem("max_step")
        consts_set = sem("consts_set")
        ranks_ready = sem("ranks_ready")
        samples_marked = sem("samples_marked")
        samples_counted = sem("samples_counted")
        blk_ready = sem("blk_ready")
        blk_loaded = [sem(f"blk_loaded{s}") for s in range(BLK_RING)]
        blk_used = sem("blk_used")
        centred = sem("centred")
        squared = sem("squared")
        var_ready = sem("var_ready")
        sd_ready = sem("sd_ready")
        h_ready = sem("h_ready")
        ht_ps = sem("ht_ps")
        ht_ready = sem("ht_ready")
        ab_ps = sem("ab_ps")
        a_ready = sem("a_ready")
        b_ready = sem("b_ready")
        w1_ready = sem("w1_ready")
        b_stored = sem("b_stored")
        a_stored = sem("a_stored")
        scatter_ready = sem("scatter_ready")
        a_scattered = sem("a_scattered")
        lane_idx_ready = sem("lane_idx_ready")
        first_count = sem("first_count")
        fill_init = sem("fill_init")
        diag_ready = sem("diag_ready")
        caps_ps = sem("caps_ps")
        caps_ready = sem("caps_ready")
        same_ready = sem("same_ready")
        src_first = sem("src_first")
        chunk_open = sem("chunk_open")
        src_loaded = [sem(f"src_loaded{s}") for s in range(RING)]
        gathered = [sem(f"gathered{s}") for s in range(RING)]
        a_loaded = [sem(f"a_loaded{s}") for s in range(AE_RING)]
        a_free = sem("a_free")
        keep_ready = sem("keep_ready")
        z_ready = sem("z_ready")
        z_turned = sem("z_turned")
        relu_done = sem("relu_done")
        messages = sem("messages")
        state_ready = sem("state_ready")
        state_stored = [sem(f"state_stored{s}") for s in range(2)]
        last_turned = sem("last_turned")
        carry_ready = sem("carry_ready")
        carry_turned = sem("carry_turned")
        head_loaded = sem("head_loaded")
        head_ready = sem("head_ready")
        head_stored = sem("head_stored")
        maxima_preset = sem("maxima_preset")
        maxima = [sem(f"maxima{g}") for g in range(NJ // BATCH)]
        x_again = sem("x_again")
        out_ready = sem("out_ready")
        out_stored = sem("out_stored")

        x_nodes = x.rearrange("(p j) c -> p j c", p=NP)
        out_nodes = out.rearrange("(p j) c -> p j c", p=NP)
        a_nodes = a_table.rearrange("(p j) c -> p j c", p=NP)
        b_nodes = b_table.rearrange("(p j) c -> p j c", p=NP)
        src_lanes = src.rearrange("(p t) -> p t", p=P)
        dst_lanes = dst.rearrange("(p t) -> p t", p=P)
        dst_blocks = dst.rearrange("(b k) -> b k", k=BLOCK)
        a_lanes = a_edges.rearrange("(p t) c -> p (t c)", p=P)
        state_lanes = states.rearrange("(p t) c -> p (t c)", p=P)

        def at(index, column):
            return bass.IndirectOffsetOnAxis(ap=index[:, column:column + 1], axis=0)

        def pairs(tiles):
            return [(k, min(2, tiles - k)) for k in range(0, tiles, 2)]

        def groups(tiles):
            return [(g, min(GROUP, tiles - g * GROUP)) for g in range((tiles + GROUP - 1) // GROUP)]

        block = ctx.enter_context(nc.Block())

        @block.sync
        def _(sp):
            for q in range(PIECES):
                sp.dma_start(xs[0:NP, q * PJ:(q + 1) * PJ, :],
                             x_nodes[:, q * PJ:(q + 1) * PJ, :]).then_inc(x_loaded[q], 16)
            sp.dma_start(b1_rows[0:NP, :], b1.rearrange("(o c) -> o c", o=1).to_broadcast((NP, C))
                         ).then_inc(weights_loaded, 16)
            sp.dma_start(b2_rows[0:NP, :], b2.rearrange("(o c) -> o c", o=1).to_broadcast((NP, C))
                         ).then_inc(weights_loaded, 16)
            sp.wait_ge(w2_cleared, 1)
            for h in range(2):
                sp.dma_start(w2_diag[h * C:(h + 1) * C, h, :], W2).then_inc(w2_loaded, 16)
            sp.dma_start(src_idx[:, :, :].rearrange("p r k -> p (r k)"),
                         src_lanes[:, 0:RING * CHUNK]).then_inc(src_first, 16)
            sp.dma_start(dst_all[:, 1:], dst_lanes).then_inc(dst_loaded, 16)

            zero_row = state[:, :, :].rearrange("p s w -> p (s w)")[:, 0:ZW].rearrange(
                "p (r w) -> p r w", r=1).to_broadcast((P, ZREP, ZW))
            sp.wait_ge(zero_row_set, 1)
            store_b = {5 + 2 * q: q for q in range(PIECES)}
            store_a = {18 + q: q for q in range(PIECES)}

            def clear(z, half, turn):
                if turn is not None:
                    sp.wait_ge(zeros_stored[half], turn)
                sp.dma_start(a_lanes[:, bass.ds(z * ZW * ZREP, ZW * ZREP)].rearrange("p (r w) -> p r w", w=ZW),
                             zero_row).then_inc(zeros_stored[half], 16)

            BUSY = 24
            for z in range(BUSY):
                clear(z, z % 2, 16 * (z // 2) if z >= 2 else None)
                if z in store_b:
                    q = store_b[z]
                    sp.wait_ge(b_ready, (q + 1) * PJ // 4)
                    sp.dma_start(b_nodes[:, q * PJ:(q + 1) * PJ, :],
                                 xs[0:NP, q * PJ:(q + 1) * PJ, :]).then_inc(b_stored, 16)
                if z in store_a:
                    q = store_a[z]
                    sp.wait_ge(a_ready, (q + 1) * PJ // 4)
                    sp.dma_start(a_nodes[:, q * PJ:(q + 1) * PJ, :],
                                 a_rows[0:NP, q * PJ:(q + 1) * PJ, :]).then_inc(a_stored, 16)
            with sp.Fori(BUSY // 2, ZEROS // 2) as i:
                for half in range(2):
                    clear(i * 2 + half, half, i * 16)
            sp.wait_ge(b_stored, 16 * PIECES)
            sp.dma_start(xs[0:NP, :, :], x_nodes).then_inc(x_again, 16)
            for half in range(2):
                sp.wait_ge(zeros_stored[half], 16 * ZEROS // 2)
            sp.wait_ge(a_scattered, 16 * NJ)

            def load_a(c, k, tiles=CHUNK):
                sp.wait_ge(a_free, c + 1)
                sp.dma_start(a_fill[:, k % AE_RING, 0:tiles * C],
                             a_lanes[:, bass.ds(c * W, tiles * C)]).then_inc(a_loaded[k % AE_RING], 16)

            with sp.Fori(0, ITERS - 1) as i:
                for k in range(RING):
                    load_a(i * RING + k, k)
                    sp.wait_ge(gathered[k], (i + 1) * GATHER)
                    sp.dma_start(src_idx[:, k, :], src_lanes[:, bass.ds((i * RING + RING + k) * CHUNK, CHUNK)]
                                 ).then_inc(src_loaded[k], 16)
            for k in range(RING):
                load_a((ITERS - 1) * RING + k, k)
                if k == 0:
                    sp.wait_ge(gathered[0], ITERS * GATHER)
                    sp.dma_start(src_idx[:, 0, 0:TAIL], src_lanes[:, CHUNKS * CHUNK:TILES]
                                 ).then_inc(src_loaded[0], 16)
            load_a(CHUNKS, RING, TAIL)
            for g in range(NJ // BATCH):
                sp.wait_ge(out_ready, g + 1)
                sp.dma_start(out_nodes[:, g * BATCH:(g + 1) * BATCH, :],
                             a_rows[0:NP, g * BATCH:(g + 1) * BATCH, :]).then_inc(out_stored, 16)
            sp.wait_ge(out_stored, 16 * (NJ // BATCH))

        @block.gpsimd
        def _(pool):
            nc.gpsimd.iota(rank_i[:, :], pattern=[[1, P + 1]], base=0, channel_multiplier=0).then_inc(pool_ranks, 1)
            nc.gpsimd.iota(nid_i[0:NP, :], pattern=[[1, SEARCHES]], base=0, channel_multiplier=NJ).then_inc(pool_const, 1)
            nc.gpsimd.memset(ones[:, :], 1.0).then_inc(pool_step, 1)
            nc.gpsimd.memset(ident[:, :], 0.0).then_inc(pool_step, 1)
            nc.gpsimd.iota(lane_i[:, 0:1], pattern=[[0, 1]], base=-1, channel_multiplier=TILES).then_inc(pool_const, 1)
            pool.wait_ge(pool_step, 2)
            nc.gpsimd.affine_select(out=ident[:, :], in_=ident[:, :], compare_op=ALU.not_equal, fill=1.0, base=0,
                                    pattern=[[-1, P]], channel_multiplier=1).then_inc(pool_const, 1)

            def gather_chunk(slot, tiles=CHUNK):
                for t in range(tiles):
                    nc.gpsimd.indirect_dma_start(
                        out=rows[:, slot, t * C:(t + 1) * C], out_offset=None,
                        in_=b_table, in_offset=at(src_idx[:, slot, :], t)).then_inc(gathered[slot], 16)

            def search(a, b):
                for j in range(a, min(b, SEARCHES)):
                    if j >= BLK_RING:
                        pool.wait_ge(blk_used, j - BLK_RING + 1)
                    nc.gpsimd.indirect_dma_start(
                        out=blocks[0:NP, j % BLK_RING, :], out_offset=None,
                        in_=dst_blocks, in_offset=at(blk_idx[0:NP, :], j)).then_inc(blk_loaded[j % BLK_RING], 16)

            pool.wait_ge(blk_ready, 1)
            search(0, SEARCHES)
            pool.wait_ge(src_first, 16)
            pool.wait_ge(b_stored, 16 * PIECES)
            for c in range(RING):
                if c == BLOCKS_AT:
                    pool.wait_ge(blk_used, SEARCHES)
                gather_chunk(c)
            pool.wait_ge(lane_idx_ready, 1)
            pool.wait_ge(a_stored, 16 * PIECES)
            pool.wait_ge(scatter_ready, 1)
            for half in range(2):
                pool.wait_ge(zeros_stored[half], 16 * ZEROS // 2)
            nc.gpsimd.indirect_dma_start(
                out=a_fill[:, AE_RING - 1, W - C:W], out_offset=None,
                in_=a_table, in_offset=at(dst_all[:, :], 1)).then_inc(fill_init, 16)
            for j in range(NJ):
                nc.gpsimd.indirect_dma_start(
                    out=a_edges, out_offset=at(first_idx[0:NP, :], j), in_=a_rows[0:NP, j, :], in_offset=None,
                    bounds_check=E - 1, oob_is_err=False).then_inc(a_scattered, 16)
            with pool.Fori(1, ITERS) as i:
                for k in range(RING):
                    pool.wait_ge(z_turned, (i * RING + k - RING + 1) * GROUPS)
                    pool.wait_ge(src_loaded[k], i * 16)
                    pool.sem_inc(chunk_open, 1)
                    gather_chunk(k)
            pool.wait_ge(z_turned, (CHUNKS - RING + 1) * GROUPS)
            pool.wait_ge(src_loaded[0], ITERS * 16)
            gather_chunk(0, TAIL)

            pool.wait_ge(state_stored[0], 16 * (CHUNKS // 2 + 2))
            pool.wait_ge(state_stored[1], 16 * (CHUNKS // 2 + 1))
            nc.gpsimd.indirect_dma_start(
                out=head[:, :], out_offset=None, in_=states, in_offset=at(lane_i, 1)).then_inc(head_loaded, 16)
            pool.wait_ge(head_ready, 1)
            nc.gpsimd.indirect_dma_start(
                out=states, out_offset=at(lane_i, 1), in_=head_new[:, :], in_offset=None).then_inc(head_stored, 16)
            pool.wait_ge(head_stored, 16)
            pool.wait_ge(maxima_preset, 1)
            for j in range(NJ):
                nc.gpsimd.indirect_dma_start(
                    out=a_rows[0:NP, j, :], out_offset=None, in_=states, in_offset=at(last_idx[0:NP, :], j),
                    bounds_check=E - 1, oob_is_err=False).then_inc(maxima[j // BATCH], 16)

        @block.scalar
        def _(act):
            act.dma_start(smp_i[0:NP, :], dst_blocks[:, 0:1].rearrange("(p m) o -> p (m o)", p=NP),
                          allow_slow_non_contiguous=True).then_inc(samples_loaded, 16)
            act.dma_start(dst_all[1:P, 0:1], dst_lanes[0:P - 1, TILES - 1:TILES],
                          allow_slow_non_contiguous=True).then_inc(dst_loaded, 16)
            for h in range(2):
                act.dma_start(w1_raw[h * C:(h + 1) * C, :, :],
                              W1.rearrange("(h c) n -> c h n", h=2)).then_inc(weights_loaded, 16)

            counted = [0]

            def count_blocks(until):
                for j in range(counted[0], until):
                    act.wait_ge(blk_loaded[j % BLK_RING], 16 * (j // BLK_RING + 1))
                    if j >= 2:
                        act.wait_ge(blk_used, j - 1)
                    nc.scalar.activation(junk_act[0:NP, j % 2 * BLOCK:(j % 2 + 1) * BLOCK], blocks[0:NP, j % BLK_RING, :],
                                         ACT.Sign, scale=-1.0, bias=nid_half[0:NP, j:j + 1],
                                         accum_out=below[0:NP, j:j + 1]).then_inc(blk_used, 1)
                counted[0] = until

            def square(q):
                act.wait_ge(centred, q + 1)
                if q >= 1:
                    act.wait_ge(var_ready, q)
                nc.scalar.activation(squares[0:NP, :], xs[0:NP, q * PJ:(q + 1) * PJ, :].rearrange("p j c -> p (j c)"),
                                     ACT.Square).then_inc(squared, 1)

            def deviation(q):
                act.wait_ge(var_ready, q + 1)
                nc.scalar.activation(stat[0:NP, q, 3, :], stat[0:NP, q, 2, :], ACT.Sqrt, scale=1.0 / C,
                                     bias=eps[0:NP, :]).then_inc(sd_ready, 1)

            def evacuate(g):
                if g < NJ // 4:
                    act.wait_ge(ht_ps, g + 1)
                    if g >= 2:
                        act.wait_ge(ab_ps, g - 1)
                    nc.scalar.activation(ht[:, g % 2, 0:2 * NP], ps_t[:, g % 2, 0:2 * NP], ACT.Relu).then_inc(ht_ready, 1)
                if g >= 1:
                    act.wait_ge(a_ready, g)
                    nc.scalar.activation(xs[0:NP, 4 * (g - 1):4 * g, :],
                                         ps_m[0:NP, (g - 1) % 2, :].rearrange("p (j w) -> p j w", j=4)[:, :, C:2 * C],
                                         ACT.Copy).then_inc(b_ready, 1)

            act.wait_ge(consts_set, 1)
            for q in range(PIECES):
                square(q)
                count_blocks(6 * q)
                if q >= 1:
                    deviation(q - 1)
            deviation(PIECES - 1)
            for g in range(NJ // 4 + 1):
                evacuate(g)
                count_blocks(max(counted[0], 6 * PIECES + g - 2))
            count_blocks(SEARCHES)

            act.wait_ge(blk_used, SEARCHES)
            act.wait_ge(lane_idx_ready, 1)
            nc.scalar.activation(junk_act[:, 0:TILES], dst_all[:, 1:], ACT.Sign, scale=-1.0, bias=lane[:, 0:1],
                                 accum_out=lane[:, 1:2]).then_inc(first_count, 1)

            def flags(c, k, tiles=CHUNK):
                now = same[:, bass.ds(c * CHUNK, CHUNK)]
                nc.scalar.activation(keep[:, k % KEEP, 0, :], now, ACT.Relu)
                nc.scalar.activation(keep[:, k % KEEP, 1, :], now, ACT.Copy, scale=FLT_MAX).then_inc(keep_ready, 1)

            def step(c, k, tiles=CHUNK):
                if tiles == CHUNK:
                    flags(c + 1, k + 1)
                for g, n in groups(tiles):
                    act.wait_ge(z_turned, c * GROUPS + g + 1)
                    full = n // 2 * P
                    last = nc.scalar.activation(zt[:, g, 0:full], ps_t[:, g, 0:full], ACT.Relu)
                    if n % 2:
                        last = nc.scalar.activation(zt[0:C, g, full:full + P], ps_t[0:C, g, full:full + P], ACT.Relu)
                    last.then_inc(relu_done, 1)
                act.wait_ge(state_ready, c + 1)
                act.dma_start(state_lanes[:, bass.ds(c * W, tiles * C)], state[:, k % 2, 0:tiles * C]
                              ).then_inc(state_stored[k % 2], 16)

            act.wait_ge(same_ready, 1)
            flags(0, 0)
            for half in range(2):
                act.sem_inc(state_stored[half], 16)
            with act.Fori(0, ITERS) as i:
                for k in range(RING):
                    step(i * RING + k, k)
            step(CHUNKS, 0, TAIL)
            act.wait_ge(state_stored[0], 16 * (CHUNKS // 2 + 2))
            act.wait_ge(state_stored[1], 16 * (CHUNKS // 2 + 1))

        @block.tensor
        def _(pe):
            pe.wait_ge(samples_marked, 1)
            for m in range(SCOLS):
                nc.tensor.matmul(ps_s[0:NP, 0, 0:SEARCHES], above[0:NP, m, 0:NP], ones_b[0:NP, :], start=m == 0, stop=False)
                last = nc.tensor.matmul(ps_s[0:NP, 0, 0:SEARCHES], inside[0:NP, m, 0:NP], column[0:NP, m, :],
                                        start=False, stop=m == SCOLS - 1)
            last.then_inc(samples_counted, 1)
            pe.wait_ge(pool_const, 3)

            def turn_h(g):
                if 4 * g % PJ == 0:
                    pe.wait_ge(h_ready, 4 * g // PJ + 1)
                if g >= 2:
                    pe.wait_ge(ht_ready, g - 1)
                for a in range(2):
                    last = nc.tensor.transpose(ps_t[:, g % 2, a * NP:(a + 1) * NP],
                                               xs[0:NP, 4 * g + 2 * a:4 * g + 2 * a + 2, :].rearrange("p j c -> p (j c)"),
                                               ident[0:NP, 0:NP])
                last.then_inc(ht_ps, 1)

            def products(g):
                pe.wait_ge(ht_ready, g + 1)
                if g >= 2:
                    pe.wait_ge(a_ready, g - 1)
                    pe.wait_ge(b_ready, g - 1)
                for a in range(2):
                    last = nc.tensor.matmul(ps_m[0:NP, g % 2, a * 2 * P:(a + 1) * 2 * P], ht[:, g % 2, a * NP:(a + 1) * NP],
                                            w1_diag[:, :, :, :].rearrange("p h w n -> p (h w n)"), start=True, stop=True)
                last.then_inc(ab_ps, 1)

            pe.wait_ge(w1_ready, 4)
            for g in range(NJ // 4 + 1):
                if g < NJ // 4:
                    turn_h(g)
                if g >= 1:
                    products(g - 1)

            pe.wait_ge(blk_ready, 1)
            pe.wait_ge(diag_ready, 1)
            for f in range(2):
                last = nc.tensor.matmul(ps_s[0:C, 0, f * P:(f + 1) * P], ones[:, 0:C], diag[:, f, :], start=True, stop=True)
            last.then_inc(caps_ps, 1)
            pe.wait_ge(w2_loaded, 32)
            pe.wait_ge(a_ready, NJ // 4)
            pe.wait_ge(b_ready, NJ // 4)

            w2_pair = w2_diag[:, :, :].rearrange("p h n -> p (h n)")

            def step(c, slot, tiles=CHUNK):
                for g, n in groups(tiles):
                    pe.wait_ge(z_ready, c * GROUPS + g + 1)
                    for k, m in pairs(n):
                        t = g * GROUP + k
                        last = nc.tensor.transpose(ps_t[0:m * C, g, k * C:k * C + P],
                                                   rows[:, slot, t * C:(t + m) * C], ident[:, :])
                    last.then_inc(z_turned, 1)
                for g, n in groups(tiles):
                    pe.wait_ge(relu_done, c * GROUPS + g + 1)
                    for k, m in pairs(n):
                        last = nc.tensor.matmul(ps_m[:, g, k * C:(k + m) * C], zt[0:m * C, g, k * C:k * C + P],
                                                w2_pair[0:m * C, 0:m * C], start=True, stop=True)
                    last.then_inc(messages, 1)

            with pe.Fori(0, ITERS) as i:
                for k in range(RING):
                    step(i * RING + k, k)
            step(CHUNKS, 0, TAIL)

            pe.wait_ge(state_ready, CHUNKS + 1)
            pe.wait_ge(caps_ready, 1)
            nc.tensor.transpose(ps_s[0:C, 0, 0:P], state[:, 0, (TAIL - 1) * C:TAIL * C], ident[:, :]).then_inc(last_turned, 1)
            pe.wait_ge(carry_ready, 1)
            nc.tensor.transpose(ps_s[:, 1, 0:C], carry_cap[:, :], ident[0:C, 0:C]).then_inc(carry_turned, 1)

        @block.vector
        def _(dve):
            steps = [0]

            def link(instruction):
                steps[0] += 1
                instruction.then_inc(dve_step, 1)
                dve.wait_ge(dve_step, steps[0])

            nc.vector.memset(w2_diag[:, :, :], 0.0).then_inc(w2_cleared, 1)
            nc.vector.memset(state[:, :, :], 0.0).then_inc(zero_row_set, 1)
            nc.vector.memset(eps[:, :], EPS)
            link(nc.vector.memset(w1_diag[:, :, :, :], 0.0))
            nc.vector.memset(ones_b[:, :], 1.0)
            nc.vector.memset(same[:, TILES:], 0.0)
            nc.vector.memset(dst_all[0:1, 0:1], -1)
            dve.wait_ge(pool_ranks, 1)
            link(nc.vector.tensor_copy(rank[:, :], rank_i[:, :]))
            link(nc.vector.tensor_scalar(base[:, :], rank[:, 0:P], float(NJ), None, ALU.mult))
            dve.wait_ge(samples_loaded, 16)
            link(nc.vector.tensor_copy(smp[0:NP, 0, :], smp_i[0:NP, :]))
            for m in range(SCOLS):
                last = nc.vector.tensor_scalar(above[0:NP, m, 0:NP], base[0:NP, 0:NP], smp[0:NP, 0, m:m + 1], None, ALU.is_gt)
            link(last)
            link(nc.vector.tensor_reduce(smp[0:NP, 1, :], above[0:NP, :, 0:NP], AX_X, ALU.add))
            link(nc.vector.tensor_scalar(smp[0:NP, 2, :], smp[0:NP, 1, :], -1.0, float(NP - 1), ALU.mult, ALU.add))
            link(nc.vector.scalar_tensor_tensor(smp[0:NP, 3, :], smp[0:NP, 2, :], -float(NJ), smp[0:NP, 0, :],
                                                ALU.mult, ALU.add))
            for m in range(SCOLS):
                nc.vector.tensor_scalar(inside[0:NP, m, 0:NP], rank[0:NP, 0:NP], smp[0:NP, 2, m:m + 1], None, ALU.is_equal)
                last = nc.vector.tensor_scalar(column[0:NP, m, :], rank[0:NP, 0:SEARCHES], smp[0:NP, 3, m:m + 1], None,
                                               ALU.is_gt)
            last.then_inc(samples_marked, 1)
            dve.wait_ge(pool_const, 3)
            nc.vector.tensor_scalar(nid_half[0:NP, :], nid_i[0:NP, :], -0.5, None, ALU.add).then_inc(consts_set, 1)
            dve.wait_ge(samples_counted, 1)
            link(nc.vector.tensor_scalar(blk[0:NP, :], ps_s[0:NP, 0, 0:SEARCHES], -1.0, 0.0, ALU.add, ALU.max))
            nc.vector.tensor_copy(blk_idx[0:NP, :], blk[0:NP, :]).then_inc(blk_ready, 1)
            dve.wait_ge(weights_loaded, 64)
            for h in range(2):
                half = slice(h * C, (h + 1) * C)
                nc.vector.tensor_tensor(w1_diag[half, h, 0, :], w1_raw[half, 0, :], w1_raw[half, 1, :],
                                        ALU.subtract).then_inc(w1_ready, 1)
                nc.vector.tensor_copy(w1_diag[half, h, 1, :], w1_raw[half, 1, :]).then_inc(w1_ready, 1)

            def piece(q):
                return xs[0:NP, q * PJ:(q + 1) * PJ, :]

            def spread(values):
                return values.rearrange("p (j o) -> p j o", o=1).to_broadcast((NP, PJ, C))

            def centre(q):
                dve.wait_ge(x_loaded[q], 16)
                s = stat[0:NP, q, :, :]
                link(nc.vector.tensor_reduce(s[:, 0, :], piece(q), AX_X, ALU.add))
                link(nc.vector.tensor_scalar(s[:, 1, :], s[:, 0, :], 1.0 / C, None, ALU.mult))
                nc.vector.tensor_tensor(piece(q), piece(q), spread(s[:, 1, :]), ALU.subtract).then_inc(centred, 1)

            def scale(q):
                s = stat[0:NP, q, :, :]
                dve.wait_ge(squared, q + 1)
                nc.vector.tensor_reduce(s[:, 2, :], squares[0:NP, :].rearrange("p (j c) -> p j c", c=C),
                                        AX_X, ALU.add).then_inc(var_ready, 1)
                dve.wait_ge(sd_ready, q + 1)
                link(nc.vector.reciprocal(s[:, 4, :], s[:, 3, :]))
                nc.vector.tensor_tensor(piece(q), piece(q), spread(s[:, 4, :]), ALU.mult).then_inc(h_ready, 1)

            for q in range(PIECES + 1):
                if q < PIECES:
                    centre(q)
                if q >= 1:
                    scale(q - 1)
            def lanes():
                dve.wait_ge(dst_loaded, 32)
                nc.vector.tensor_scalar(lane[:, 0:1], dst_all[:, 1:2], 0.5, None, ALU.add).then_inc(lane_idx_ready, 1)
                link(nc.vector.tensor_tensor(same[:, 0:TILES], dst_all[:, 1:], dst_all[:, 0:TILES], ALU.is_equal))
                link(nc.vector.tensor_tensor(lane[:, 2:3], dst_all[:, 1:2], dst_all[:, TILES:TILES + 1], ALU.is_equal))
                link(nc.vector.tensor_tensor(lane[:, 3:4], lane[:, 2:3], same[:, 0:1], ALU.mult))
                dve.wait_ge(pool_const, 3)
                nc.vector.tensor_scalar(diag[:, 0, :], ident[:, :], same[:, 0:1], None, ALU.mult)
                nc.vector.tensor_scalar(diag[:, 1, :], ident[:, :], lane[:, 3:4], None, ALU.mult).then_inc(diag_ready, 1)
                dve.wait_ge(diag_ready, 1)
                nc.vector.tensor_scalar(same[:, 0:TILES], same[:, 0:TILES], 2.0, -1.0, ALU.mult, ALU.add).then_inc(same_ready, 1)
                dve.wait_ge(caps_ps, 1)
                link(nc.vector.tensor_scalar(caps[:, :, :].rearrange("p f q -> p (f q)"), ps_s[0:C, 0, 0:2 * P],
                                             2.0, -1.0, ALU.mult, ALU.add))
                link(nc.vector.tensor_scalar(caps[:, :, :], caps[:, :, :], FLT_MAX, None, ALU.mult))

            for g in range(NJ // 4):
                dve.wait_ge(ab_ps, g + 1)
                nc.vector.tensor_tensor(a_rows[0:NP, 4 * g:4 * g + 4, :],
                                        ps_m[0:NP, g % 2, :].rearrange("p (j w) -> p j w", j=4)[:, :, 0:C],
                                        b1_rows[0:NP, :].rearrange("p (o c) -> p o c", o=1).to_broadcast((NP, 4, C)),
                                        ALU.add).then_inc(a_ready, 1)
            lanes()
            dve.wait_ge(blk_used, SEARCHES)
            link(nc.vector.tensor_scalar(below[0:NP, :], below[0:NP, :], 0.5, BLOCK / 2.0, ALU.mult, ALU.add))
            link(nc.vector.scalar_tensor_tensor(first[0:NP, :], blk[0:NP, :], float(BLOCK), below[0:NP, :], ALU.mult, ALU.add))
            link(nc.vector.tensor_tensor(empty[0:NP, :], first[0:NP, 0:NJ], first[0:NP, 1:SEARCHES], ALU.is_equal))
            nc.vector.scalar_tensor_tensor(first_idx[0:NP, :], empty[0:NP, :], OUT_OF_RANGE, first[0:NP, 0:NJ],
                                           ALU.mult, ALU.add).then_inc(scatter_ready, 1)
            link(nc.vector.tensor_scalar(tmp_n[0:NP, :], first[0:NP, 1:SEARCHES], -1.0, 0.0, ALU.add, ALU.max))
            nc.vector.scalar_tensor_tensor(last_idx[0:NP, :], empty[0:NP, :], OUT_OF_RANGE, tmp_n[0:NP, :],
                                           ALU.mult, ALU.add)

            dve.wait_ge(first_count, 1)
            link(nc.vector.tensor_scalar(lane[:, 4:5], lane[:, 1:2], float(TILES), 0.5, ALU.add, ALU.mult))
            link(nc.vector.tensor_copy(lane[:, 5:6], lane_i[:, 0:1]))
            nc.vector.tensor_tensor(lane_i[:, 1:2], lane[:, 4:5], lane[:, 5:6], ALU.add).then_inc(caps_ready, 1)

            for half in range(2):
                dve.wait_ge(zeros_stored[half], 16 * ZEROS // 2)
            nc.vector.memset(state[:, 1, W - C:W], -FLT_MAX).then_inc(a_free, AE_RING - 1)
            dve.wait_ge(a_scattered, 16 * NJ)
            nc.vector.tensor_scalar(a_rows[0:NP, :, :], b2_rows[0:NP, :].rearrange("p (o c) -> p o c", o=1)
                                    .to_broadcast((NP, NJ, C)), -1.0, None, ALU.mult).then_inc(maxima_preset, 1)
            dve.wait_ge(fill_init, 16)
            dve.wait_ge(a_free, AE_RING - 1)

            def fill(c, k, i):
                i, k = (i + 1, 0) if k == RING else (i, k)
                slot = k % AE_RING
                dve.wait_ge(a_loaded[slot], (i * (RING // AE_RING) + k // AE_RING + 1) * 16)
                dve.wait_ge(keep_ready, c + 1)
                for t in range(CHUNK):
                    if t == 0:
                        before = a_fill[:, (slot - 1) % AE_RING, W - C:W]
                    else:
                        before = a_fill[:, slot, (t - 1) * C:t * C]
                        dve.wait_ge(fill_step, c * CHUNK + t)
                    here = a_fill[:, slot, t * C:(t + 1) * C]
                    nc.vector.scalar_tensor_tensor(here, before, keep[:, k % KEEP, 0, t:t + 1], here,
                                                   ALU.mult, ALU.add).then_inc(fill_step, 1)
                    if t == 0:
                        dve.wait_ge(fill_step, c * CHUNK + 1)
                        dve.sem_inc(a_free, 1)

            def add(c, k, i, tiles=CHUNK):
                dve.wait_ge(fill_step, (c + 1) * CHUNK)
                dve.wait_ge(gathered[k], i * GATHER + 16 * tiles)
                for g, n in groups(tiles):
                    part = slice(g * GROUP * C, (g * GROUP + n) * C)
                    nc.vector.tensor_tensor(rows[:, k, part], rows[:, k, part], a_fill[:, k % AE_RING, part],
                                            ALU.add).then_inc(z_ready, 1)

            def maximum(c, k, i, tiles=CHUNK):
                half = k % 2
                dve.wait_ge(state_stored[half], (i * (RING // 2) + k // 2 + 1) * 16)
                for t in range(tiles):
                    g, r = divmod(t, GROUP)
                    if r == 0:
                        dve.wait_ge(messages, c * GROUPS + g + 1)
                    if t == 0:
                        before = state[:, 1 - half, W - C:W]
                    else:
                        before = state[:, half, (t - 1) * C:t * C]
                        dve.wait_ge(max_step, c * CHUNK + t)
                    nc.vector.scalar_tensor_tensor(state[:, half, t * C:(t + 1) * C], before,
                                                   keep[:, k % KEEP, 1, t:t + 1], ps_m[:, g, r * C:(r + 1) * C],
                                                   ALU.min, ALU.max).then_inc(max_step, 1)
                dve.wait_ge(max_step, c * CHUNK + tiles)
                dve.sem_inc(state_ready, 1)

            fill(0, 0, 0)
            with dve.Fori(0, ITERS) as i:
                for k in range(RING):
                    c = i * RING + k
                    add(c, k, i)
                    fill(c + 1, k + 1, i)
                    maximum(c, k, i)
            add(CHUNKS, 0, ITERS, TAIL)
            maximum(CHUNKS, 0, ITERS, TAIL)

            dve.wait_ge(last_turned, 1)
            nc.vector.memset(carry[:, 0:1], -FLT_MAX)
            link(nc.vector.tensor_tensor_scan(carry[:, 1:P], caps[:, 1, 0:P - 1], ps_s[0:C, 0, 0:P - 1], -FLT_MAX,
                                              ALU.min, ALU.max))
            nc.vector.tensor_tensor(carry_cap[:, :], carry[:, :], caps[:, 0, :], ALU.min).then_inc(carry_ready, 1)
            dve.wait_ge(carry_turned, 1)
            dve.wait_ge(head_loaded, 16)
            nc.vector.tensor_tensor(head_new[:, :], head[:, :], ps_s[:, 1, 0:C], ALU.max).then_inc(head_ready, 1)

            dve.wait_ge(x_again, 16)
            for g in range(NJ // BATCH):
                dve.wait_ge(maxima[g], 16 * BATCH)
                part = a_rows[0:NP, g * BATCH:(g + 1) * BATCH, :]
                link(nc.vector.tensor_tensor(part, part, b2_rows[0:NP, :].rearrange("p (o c) -> p o c", o=1)
                                             .to_broadcast((NP, BATCH, C)), ALU.add))
                nc.vector.tensor_tensor(part, part, xs[0:NP, g * BATCH:(g + 1) * BATCH, :], ALU.add).then_inc(out_ready, 1)


_INS = ["x", "src", "dst", "L0_gnn_W1", "L0_gnn_b1", "L0_gnn_W2", "L0_gnn_b2"]


def kernel(**inputs):
    import numpy as _np
    import concourse.bacc as _bacc
    from concourse import mybir as _mybir
    from concourse.bass_utils import run_bass_kernel_spmd as _run

    nc = _bacc.Bacc("TRN2", target_bir_lowering=False, num_devices=1)
    arrays, args = {}, []
    for name in _INS:
        a = _np.ascontiguousarray(inputs[name])
        arrays[f"in_{name}_dram"] = a
        args.append(nc.dram_tensor(f"in_{name}_dram", a.shape, _mybir.dt.from_np(a.dtype), kind="ExternalInput").ap())
    shape = arrays["in_x_dram"].shape
    args.append(nc.dram_tensor("out_dram", shape, _mybir.dt.float32, kind="ExternalOutput").ap())
    edge_conv(nc, *args)
    r = _run(nc, [arrays], core_ids=[0])
    return r.results[0]["out_dram"]
```

```python
from contextlib import ExitStack

import concourse.bass as bass
from concourse import mybir

F32 = mybir.dt.float32
BF16 = mybir.dt.bfloat16
FP16 = mybir.dt.float16
I32 = mybir.dt.int32
ALU = mybir.AluOpType
ACT = mybir.ActivationFunctionType
AX_X = mybir.AxisListType.X

FLT_MAX = 3.4028234663852886e38
EPS = 1e-5
P = 128


def edge_conv(nc, x, src, dst, W1, b1, W2, b2, out):
    N, C = x.shape
    E = src.shape[0]
    TILES = E // P
    CHUNK = 12
    RING = 26
    ITERS = TILES // (CHUNK * RING)
    CHUNKS = ITERS * RING
    TAIL = TILES - CHUNKS * CHUNK
    assert E == P * TILES and 0 < TAIL <= 8 and TAIL % 2 == 1
    W = CHUNK * C
    GROUP = 8
    GROUPS = (CHUNK + GROUP - 1) // GROUP
    NP = 125
    NJ = N // NP
    assert NP * NJ == N
    PIECES, PJ = 5, NJ // 5
    BLOCK = 320
    SAMPLES = E // BLOCK
    SCOLS = SAMPLES // NP
    assert SCOLS * NP == SAMPLES
    BLK_RING = 23
    BATCH = 10
    SEARCHES = NJ + 1
    AE_RING = 2
    KEEP = RING // 2
    SQUARES_AT, BLOCKS_AT = RING - 15, RING - 13
    assert RING % AE_RING == 0 and RING % 2 == 0 and BLK_RING * BLOCK <= 13 * W
    ZW, ZREP = 1250, 2
    ZEROS = TILES * C // (ZW * ZREP)
    OUT_OF_RANGE = float(1 << 22)
    OCTET = 8
    PAGES = -(-N // (OCTET * P))
    PARTS = 3
    QUARTER = 32
    assert N - (PAGES - 1) * OCTET * P <= OCTET * QUARTER and PARTS * QUARTER <= P
    KEYS_AHEAD, MATCH_AHEAD, PICK_AHEAD, CHOOSE_AHEAD = 4, 3, 2, 1
    FREE = 2
    GATHERED = CHUNK - 1

    with ExitStack() as ctx:
        def sb(name, shape, dt=F32):
            return ctx.enter_context(nc.sbuf_tensor(name, shape, dt))

        def psum(name, shape, dt=F32):
            return ctx.enter_context(nc.psum_tensor(name, shape, dt))

        def sem(name):
            return ctx.enter_context(nc.semaphore(name))

        a_table = nc.dram_tensor("a_table", [N, C], F32).ap()
        b_table = nc.dram_tensor("b_table", [N, C], F32).ap()
        a_edges = nc.dram_tensor("a_edges", [E, C], F32).ap()
        states = nc.dram_tensor("states", [E, C], F32).ap()

        rows = sb("rows", [P, RING, W])
        a_fill = sb("a_fill", [P, AE_RING, W])
        state = sb("state", [P, 2, W])
        zt = sb("zt", [P, GROUPS, 512])
        src_idx = sb("src_idx", [P, RING, CHUNK], I32)
        same = sb("same", [P, TILES + CHUNK])
        keep = sb("keep", [P, KEEP, 2, CHUNK])
        dst_all = sb("dst_all", [P, TILES + 1], I32)
        shared = sb("shared", [P, PAGES * PARTS * OCTET * C // 2])
        xs = shared[:, 0:NJ * C].rearrange("p (j c) -> p j c", c=C)
        table = shared[:, :].bitcast(BF16).rearrange("p (g t w) -> p g t w", t=PARTS, w=OCTET * C)
        page = a_fill[:, :, :].rearrange("p s w -> p (s w)")[:, 0:2 * OCTET * C].rearrange(
            "p (s w) -> p s w", s=2)
        a_rows = sb("a_rows", [P, NJ, C])
        squares = rows[:, SQUARES_AT:SQUARES_AT + 2, :].rearrange("p s w -> p (s w)")[:, 0:PJ * C]
        ht = sb("ht", [P, 2, 256])
        blocks = rows[:, BLOCKS_AT:, :].rearrange("p s w -> p (s w)").bitcast(I32)[:, 0:BLK_RING * BLOCK].rearrange(
            "p (s k) -> p s k", k=BLOCK)
        junk_act = zt[:, :, :].rearrange("p g w -> p (g w)").bitcast(mybir.dt.int8)
        ident = sb("ident", [P, P])
        ones = sb("ones", [P, P])
        w1_raw = sb("w1_raw", [P, 2, C])
        w1_diag = sb("w1_diag", [P, 2, 2, C])
        w2_diag = sb("w2_diag", [P, 2, C])
        b1_rows = sb("b1_rows", [P, C])
        b2_rows = sb("b2_rows", [P, C])
        smp_i = sb("smp_i", [P, SCOLS], I32)
        smp = sb("smp", [P, 4, SCOLS])
        rank_i = sb("rank_i", [P, P + 1], I32)
        rank = sb("rank", [P, P + 1])
        base = sb("base", [P, P])
        marks = a_rows[:, :, :].rearrange("p j c -> p (j c)").bitcast(BF16)[:, 0:3 * SCOLS * P].rearrange(
            "p (k m n) -> p k m n", k=3, n=P)
        above = marks[:, 0, :, :]
        inside = marks[:, 1, :, :]
        column = marks[:, 2, :, 0:SEARCHES]
        ones_b = sb("ones_b", [P, SEARCHES], BF16)
        nid_i = sb("nid_i", [P, SEARCHES], I32)
        nid_half = sb("nid_half", [P, SEARCHES])
        blk = sb("blk", [P, SEARCHES])
        blk_idx = sb("blk_idx", [P, SEARCHES], I32)
        below = sb("below", [P, SEARCHES])
        first = sb("first", [P, SEARCHES])
        empty = sb("empty", [P, NJ])
        first_idx = sb("first_idx", [P, NJ], I32)
        last_idx = sb("last_idx", [P, NJ], I32)
        tmp_n = sb("tmp_n", [P, NJ])
        stat = sb("stat", [P, PIECES, 5, PJ])
        eps = sb("eps", [P, 1])
        lane = sb("lane", [P, 12])
        lane_i = sb("lane_i", [P, 2], I32)
        diag = sb("diag", [P, 2, P])
        caps = sb("caps", [C, 2, P])
        carry = sb("carry", [C, P])
        carry_cap = sb("carry_cap", [C, P])
        head = sb("head", [P, C])
        head_new = sb("head_new", [P, C])

        page_i = sb("page_i", [P, PAGES], I32)
        ident_h = sb("ident_h", [P, P], FP16)
        ones_h = sb("ones_h", [P, P], FP16)
        page_keys = sb("page_keys", [P, PAGES], FP16)
        octets = sb("octets", [P, OCTET])
        key_bits = sb("key_bits", [P, 2, 2], I32)
        key_octet = sb("key_octet", [P, 2, 2])
        key_is = dst_all[:, 0:PAGES * P].bitcast(BF16).rearrange(
            "p (s g e) -> p s g e", s=2, e=P)
        behind = dst_all[:, PAGES * P:PAGES * P + 2 * P + OCTET * C + RING * OCTET]
        key_diag = behind[:, 0:P].bitcast(FP16).rearrange("p (s e) -> p s e", s=2)
        key_row = behind[:, P:2 * P].bitcast(FP16).rearrange("p (s e) -> p s e", s=2)
        masked = behind[:, 2 * P:2 * P + OCTET * C].bitcast(F32).rearrange(
            "p (o c) -> p o c", c=C)
        octet_is = behind[:, 2 * P + OCTET * C:].bitcast(F32).rearrange(
            "p (k o) -> p k o", o=OCTET)

        ps_t = psum("ps_t", [P, GROUPS, 512])
        ps_m = psum("ps_m", [P, GROUPS, 512])
        ps_s = psum("ps_s", [P, 512])
        ps_g = psum("ps_g", [P, 2, 512])
        ps_k = ps_s[:, 0:P]

        x_loaded = [sem(f"x_loaded{q}") for q in range(PIECES)]
        weights_loaded = sem("weights_loaded")
        w2_loaded = sem("w2_loaded")
        samples_loaded = sem("samples_loaded")
        dst_loaded = sem("dst_loaded")
        zero_row_set = sem("zero_row_set")
        zeros_stored = [sem(f"zeros_stored{s}") for s in range(2)]
        w2_cleared = sem("w2_cleared")
        pool_const = sem("pool_const")
        pool_step = sem("pool_step")
        pool_ranks = sem("pool_ranks")
        dve_step = sem("dve_step")
        fill_step = sem("fill_step")
        max_step = sem("max_step")
        consts_set = sem("consts_set")
        samples_marked = sem("samples_marked")
        samples_counted = sem("samples_counted")
        blk_ready = sem("blk_ready")
        blk_loaded = [sem(f"blk_loaded{s}") for s in range(BLK_RING)]
        blk_used = sem("blk_used")
        centred = sem("centred")
        squared = sem("squared")
        var_ready = sem("var_ready")
        sd_ready = sem("sd_ready")
        h_ready = sem("h_ready")
        ht_ps = sem("ht_ps")
        ht_ready = sem("ht_ready")
        ab_ps = sem("ab_ps")
        a_ready = sem("a_ready")
        b_ready = sem("b_ready")
        w1_ready = sem("w1_ready")
        b_stored = sem("b_stored")
        a_stored = sem("a_stored")
        scatter_ready = sem("scatter_ready")
        a_scattered = sem("a_scattered")
        lane_idx_ready = sem("lane_idx_ready")
        first_count = sem("first_count")
        fill_init = sem("fill_init")
        diag_ready = sem("diag_ready")
        caps_ps = sem("caps_ps")
        caps_ready = sem("caps_ready")
        same_ready = sem("same_ready")
        src_first = sem("src_first")
        chunk_open = sem("chunk_open")
        src_loaded = [sem(f"src_loaded{s}") for s in range(RING // 2)]
        gathered = [sem(f"gathered{s}") for s in range(RING)]
        a_loaded = [sem(f"a_loaded{s}") for s in range(AE_RING)]
        a_free = sem("a_free")
        keep_ready = sem("keep_ready")
        z_ready = sem("z_ready")
        z_turned = sem("z_turned")
        relu_done = sem("relu_done")
        messages = sem("messages")
        state_stored = [sem(f"state_stored{s}") for s in range(2)]
        last_turned = sem("last_turned")
        carry_ready = sem("carry_ready")
        carry_turned = sem("carry_turned")
        head_loaded = sem("head_loaded")
        head_ready = sem("head_ready")
        head_stored = sem("head_stored")
        maxima_preset = sem("maxima_preset")
        maxima = [sem(f"maxima{g}") for g in range(NJ // BATCH)]
        x_again = sem("x_again")
        out_ready = sem("out_ready")
        out_stored = sem("out_stored")

        page_loaded = [sem(f"page_loaded{s}") for s in range(2)]
        page_part = sem("page_part")
        page_left = sem("page_left")
        table_ready = sem("table_ready")
        picks_set = sem("picks_set")
        keys_spread = sem("keys_spread")
        keys_turned = sem("keys_turned")
        keys_ready = sem("keys_ready")
        keys_matched = sem("keys_matched")
        picked = sem("picked")
        chosen = sem("chosen")
        bits_split = sem("bits_split")
        bits_converted = sem("bits_converted")
        octet_masked = sem("octet_masked")
        octets_marked = sem("octets_marked")

        x_nodes = x.rearrange("(p j) c -> p j c", p=NP)
        out_nodes = out.rearrange("(p j) c -> p j c", p=NP)
        a_nodes = a_table.rearrange("(p j) c -> p j c", p=NP)
        b_nodes = b_table.rearrange("(p j) c -> p j c", p=NP)
        src_lanes = src.rearrange("(p t) -> p t", p=P)
        dst_lanes = dst.rearrange("(p t) -> p t", p=P)
        dst_blocks = dst.rearrange("(b k) -> b k", k=BLOCK)
        a_lanes = a_edges.rearrange("(p t) c -> p (t c)", p=P)
        state_lanes = states.rearrange("(p t) c -> p (t c)", p=P)

        def at(index, column):
            return bass.IndirectOffsetOnAxis(ap=index[:, column:column + 1], axis=0)

        def pairs(tiles):
            return [(k, min(2, tiles - k)) for k in range(0, tiles, 2)]

        def groups(tiles):
            return [(g, min(GROUP, tiles - g * GROUP)) for g in range((tiles + GROUP - 1) // GROUP)]

        block = ctx.enter_context(nc.Block())

        @block.sync
        def _(sp):
            for q in range(PIECES):
                sp.dma_start(xs[0:NP, q * PJ:(q + 1) * PJ, :],
                             x_nodes[:, q * PJ:(q + 1) * PJ, :]).then_inc(x_loaded[q], 16)
            sp.dma_start(b1_rows[0:NP, :], b1.rearrange("(o c) -> o c", o=1).to_broadcast((NP, C))
                         ).then_inc(weights_loaded, 16)
            sp.dma_start(b2_rows[0:NP, :], b2.rearrange("(o c) -> o c", o=1).to_broadcast((NP, C))
                         ).then_inc(weights_loaded, 16)
            sp.wait_ge(w2_cleared, 1)
            for h in range(2):
                sp.dma_start(w2_diag[h * C:(h + 1) * C, h, :], W2).then_inc(w2_loaded, 16)
            sp.dma_start(src_idx[:, :, :].rearrange("p r k -> p (r k)"),
                         src_lanes[:, 0:RING * CHUNK]).then_inc(src_first, 16)
            sp.dma_start(dst_all[:, 1:], dst_lanes).then_inc(dst_loaded, 16)

            zero_row = state[:, :, :].rearrange("p s w -> p (s w)")[:, 0:ZW].rearrange(
                "p (r w) -> p r w", r=1).to_broadcast((P, ZREP, ZW))
            sp.wait_ge(zero_row_set, 1)
            store_b = {9 + 2 * q: q for q in range(PIECES)}

            def clear(z, half, turn):
                if turn is not None:
                    sp.wait_ge(zeros_stored[half], turn)
                sp.dma_start(a_lanes[:, bass.ds(z * ZW * ZREP, ZW * ZREP)].rearrange("p (r w) -> p r w", w=ZW),
                             zero_row).then_inc(zeros_stored[half], 16)

            def load_page(g):
                if g == 0:
                    sp.wait_ge(b_stored, 16 * PIECES)
                    sp.wait_ge(page_left, 1)
                if g >= 2:
                    sp.wait_ge(page_part, (g - 1) * PARTS)
                first_row = g * OCTET * P
                full = min(P, (N - first_row) // OCTET)
                part = b_table[first_row:first_row + full * OCTET, :].rearrange("(l e) c -> l (e c)", e=OCTET)
                rest = (N - first_row) % OCTET if full < P else 0
                for top in range(0, PARTS * QUARTER, QUARTER) if g == PAGES - 1 else (0,):
                    sp.dma_start(page[top:top + full, g % 2, :], part).then_inc(page_loaded[g % 2], 16)
                    if rest:
                        sp.dma_start(page[top + full:top + full + 1, g % 2, 0:rest * C],
                                     b_table[N - rest:N, :].rearrange("(o e) c -> o (e c)", o=1)
                                     ).then_inc(page_loaded[g % 2], 16)

            BUSY = 18
            for z in range(BUSY):
                clear(z, z % 2, 16 * (z // 2) if z >= 2 else None)
                if z in store_b:
                    q = store_b[z]
                    sp.wait_ge(b_ready, (q + 1) * PJ // 4)
                    sp.dma_start(b_nodes[:, q * PJ:(q + 1) * PJ, :],
                                 xs[0:NP, q * PJ:(q + 1) * PJ, :]).then_inc(b_stored, 16)
            with sp.Fori(BUSY // 2, ZEROS // 2) as i:
                for half in range(2):
                    clear(i * 2 + half, half, i * 16)
            sp.wait_ge(a_ready, NJ // 4)
            sp.dma_start(a_nodes, a_rows[0:NP, :, :]).then_inc(a_stored, 16)
            for g in range(PAGES):
                load_page(g)
            for k in range(RING // 2):
                sp.sem_inc(src_loaded[k], 32)
            for half in range(2):
                sp.wait_ge(zeros_stored[half], 16 * ZEROS // 2)
            sp.wait_ge(a_scattered, 16 * NJ)
            sp.wait_ge(page_part, PAGES * PARTS)
            sp.wait_ge(bits_split, KEYS_AHEAD)

            def load_a(c, k, tiles=CHUNK):
                sp.wait_ge(a_free, c + 1)
                sp.dma_start(a_fill[:, k % AE_RING, 0:tiles * C],
                             a_lanes[:, bass.ds(c * W, tiles * C)]).then_inc(a_loaded[k % AE_RING], 16)

            with sp.Fori(0, ITERS - 1) as i:
                for k in range(RING):
                    load_a(i * RING + k, k)
                    sp.wait_ge(gathered[k], (i + 1) * 16 * GATHERED)
                    sp.dma_start(src_idx[:, k, :], src_lanes[:, bass.ds((i * RING + RING + k) * CHUNK, CHUNK)]
                                 ).then_inc(src_loaded[k // 2], 16)
            for k in range(RING):
                load_a((ITERS - 1) * RING + k, k)
                if k == 0:
                    sp.wait_ge(gathered[0], ITERS * 16 * GATHERED)
                    sp.dma_start(src_idx[:, 0, 0:TAIL], src_lanes[:, CHUNKS * CHUNK:TILES]
                                 ).then_inc(src_loaded[0], 16)
                    sp.sem_inc(src_loaded[0], 16)
                    sp.sem_inc(src_loaded[1], 32)
            load_a(CHUNKS, RING, TAIL)
            sp.wait_ge(picked, CHUNKS + PICK_AHEAD + FREE)
            sp.wait_ge(head_stored, 16)
            sp.dma_start(xs[0:NP, :, :], x_nodes).then_inc(x_again, 16)
            for g in range(NJ // BATCH):
                sp.wait_ge(out_ready, g + 1)
                sp.dma_start(out_nodes[:, g * BATCH:(g + 1) * BATCH, :],
                             a_rows[0:NP, g * BATCH:(g + 1) * BATCH, :]).then_inc(out_stored, 16)
            sp.wait_ge(out_stored, 16 * (NJ // BATCH))

        @block.gpsimd
        def _(pool):
            nc.gpsimd.iota(rank_i[:, :], pattern=[[1, P + 1]], base=0, channel_multiplier=0).then_inc(pool_ranks, 1)
            nc.gpsimd.iota(page_i[:, :], pattern=[[P, PAGES]], base=0, channel_multiplier=1).then_inc(pool_ranks, 1)
            nc.gpsimd.iota(nid_i[0:NP, :], pattern=[[1, SEARCHES]], base=0, channel_multiplier=NJ).then_inc(pool_const, 1)
            nc.gpsimd.memset(ones[:, :], 1.0).then_inc(pool_step, 1)
            nc.gpsimd.memset(ident[:, :], 0.0).then_inc(pool_step, 1)
            nc.gpsimd.iota(lane_i[:, 0:1], pattern=[[0, 1]], base=-1, channel_multiplier=TILES).then_inc(pool_const, 1)
            pool.wait_ge(pool_step, 2)
            nc.gpsimd.affine_select(out=ident[:, :], in_=ident[:, :], compare_op=ALU.not_equal, fill=1.0, base=0,
                                    pattern=[[-1, P]], channel_multiplier=1).then_inc(pool_const, 1)

            def gather_chunk(slot, tiles=GATHERED):
                for t in range(tiles):
                    nc.gpsimd.indirect_dma_start(
                        out=rows[:, slot, t * C:(t + 1) * C], out_offset=None,
                        in_=b_table, in_offset=at(src_idx[:, slot, :], t)).then_inc(gathered[slot], 16)

            def search(a, b):
                for j in range(a, min(b, SEARCHES)):
                    if j >= BLK_RING:
                        pool.wait_ge(blk_used, j - BLK_RING + 1)
                    nc.gpsimd.indirect_dma_start(
                        out=blocks[0:NP, j % BLK_RING, :], out_offset=None,
                        in_=dst_blocks, in_offset=at(blk_idx[0:NP, :], j)).then_inc(blk_loaded[j % BLK_RING], 16)

            pool.wait_ge(blk_ready, 1)
            search(0, SEARCHES)
            pool.wait_ge(src_first, 16)
            pool.wait_ge(b_stored, 16 * PIECES)
            for c in range(RING - 1):
                if c == BLOCKS_AT:
                    pool.wait_ge(blk_used, SEARCHES)
                gather_chunk(c)
            pool.wait_ge(scatter_ready, 1)
            for half in range(2):
                pool.wait_ge(zeros_stored[half], 16 * ZEROS // 2)

            def scatter_a(a, b):
                for j in range(a, b):
                    nc.gpsimd.indirect_dma_start(
                        out=a_edges, out_offset=at(first_idx[0:NP, :], j), in_=a_rows[0:NP, j, :], in_offset=None,
                        bounds_check=E - 1, oob_is_err=False).then_inc(a_scattered, 16)

            scatter_a(0, BATCH)
            pool.wait_ge(lane_idx_ready, 1)
            pool.wait_ge(a_stored, 16)
            nc.gpsimd.indirect_dma_start(
                out=a_fill[:, AE_RING - 1, W - C:W], out_offset=None,
                in_=a_table, in_offset=at(dst_all[:, :], 1)).then_inc(fill_init, 16)
            scatter_a(BATCH, NJ)
            gather_chunk(RING - 1)
            with pool.Fori(1, ITERS) as i:
                for k in range(RING):
                    pool.wait_ge(z_turned, (i * RING + k - RING + 1) * GROUPS)
                    pool.wait_ge(src_loaded[k // 2], (i + 1) * 32)
                    pool.sem_inc(chunk_open, 1)
                    gather_chunk(k)
            pool.wait_ge(z_turned, (CHUNKS - RING + 1) * GROUPS)
            pool.wait_ge(src_loaded[0], (ITERS + 1) * 32)
            gather_chunk(0, TAIL)

            pool.wait_ge(state_stored[0], 16 * (CHUNKS // 2 + 2))
            pool.wait_ge(state_stored[1], 16 * (CHUNKS // 2 + 1))
            nc.gpsimd.indirect_dma_start(
                out=head[:, :], out_offset=None, in_=states, in_offset=at(lane_i, 1)).then_inc(head_loaded, 16)
            pool.wait_ge(head_ready, 1)
            nc.gpsimd.indirect_dma_start(
                out=states, out_offset=at(lane_i, 1), in_=head_new[:, :], in_offset=None).then_inc(head_stored, 16)
            pool.wait_ge(head_stored, 16)
            pool.wait_ge(maxima_preset, 1)
            for j in range(NJ):
                nc.gpsimd.indirect_dma_start(
                    out=a_rows[0:NP, j, :], out_offset=None, in_=states, in_offset=at(last_idx[0:NP, :], j),
                    bounds_check=E - 1, oob_is_err=False).then_inc(maxima[j // BATCH], 16)

        @block.scalar
        def _(act):
            act.dma_start(smp_i[0:NP, :], dst_blocks[:, 0:1].rearrange("(p m) o -> p (m o)", p=NP),
                          allow_slow_non_contiguous=True).then_inc(samples_loaded, 16)
            act.dma_start(dst_all[1:P, 0:1], dst_lanes[0:P - 1, TILES - 1:TILES],
                          allow_slow_non_contiguous=True).then_inc(dst_loaded, 16)
            for h in range(2):
                act.dma_start(w1_raw[h * C:(h + 1) * C, :, :],
                              W1.rearrange("(h c) n -> c h n", h=2)).then_inc(weights_loaded, 16)

            counted = [0]

            def count_blocks(until):
                for j in range(counted[0], until):
                    act.wait_ge(blk_loaded[j % BLK_RING], 16 * (j // BLK_RING + 1))
                    if j >= 2:
                        act.wait_ge(blk_used, j - 1)
                    nc.scalar.activation(junk_act[0:NP, j % 2 * BLOCK:(j % 2 + 1) * BLOCK], blocks[0:NP, j % BLK_RING, :],
                                         ACT.Sign, scale=-1.0, bias=nid_half[0:NP, j:j + 1],
                                         accum_out=below[0:NP, j:j + 1]).then_inc(blk_used, 1)
                counted[0] = until

            def square(q):
                act.wait_ge(centred, q + 1)
                if q >= 1:
                    act.wait_ge(var_ready, q)
                nc.scalar.activation(squares[0:NP, :], xs[0:NP, q * PJ:(q + 1) * PJ, :].rearrange("p j c -> p (j c)"),
                                     ACT.Square).then_inc(squared, 1)

            def deviation(q):
                act.wait_ge(var_ready, q + 1)
                nc.scalar.activation(stat[0:NP, q, 3, :], stat[0:NP, q, 2, :], ACT.Sqrt, scale=1.0 / C,
                                     bias=eps[0:NP, :]).then_inc(sd_ready, 1)

            def evacuate(g):
                if g < NJ // 4:
                    act.wait_ge(ht_ps, g + 1)
                    if g >= 2:
                        act.wait_ge(ab_ps, g - 1)
                    nc.scalar.activation(ht[:, g % 2, 0:2 * NP], ps_t[:, g % 2, 0:2 * NP], ACT.Relu).then_inc(ht_ready, 1)
                if g >= 1:
                    act.wait_ge(a_ready, g)
                    nc.scalar.activation(xs[0:NP, 4 * (g - 1):4 * g, :],
                                         ps_m[0:NP, (g - 1) % 2, :].rearrange("p (j w) -> p j w", j=4)[:, :, C:2 * C],
                                         ACT.Copy).then_inc(b_ready, 1)

            act.wait_ge(consts_set, 1)
            for q in range(PIECES):
                square(q)
                count_blocks(6 * q)
                if q >= 1:
                    deviation(q - 1)
            deviation(PIECES - 1)
            for g in range(NJ // 4 + 1):
                evacuate(g)
                count_blocks(max(counted[0], 6 * PIECES + g - 2))
            count_blocks(SEARCHES)

            act.wait_ge(blk_used, SEARCHES)
            act.wait_ge(lane_idx_ready, 1)
            nc.scalar.activation(junk_act[:, 0:TILES], dst_all[:, 1:], ACT.Sign, scale=-1.0, bias=lane[:, 0:1],
                                 accum_out=lane[:, 1:2]).then_inc(first_count, 1)

            def flags(c, k, tiles=CHUNK):
                now = same[:, bass.ds(c * CHUNK, CHUNK)]
                nc.scalar.activation(keep[:, k % KEEP, 0, :], now, ACT.Relu)
                nc.scalar.activation(keep[:, k % KEEP, 1, :], now, ACT.Copy, scale=FLT_MAX).then_inc(keep_ready, 1)

            def spread_keys(c, k):
                act.wait_ge(bits_split, c + 1)
                act.wait_ge(octets_marked, c - 1 + FREE)
                nc.scalar.activation(key_octet[:, k % 2, :], key_bits[:, k % 2, :], ACT.Copy).then_inc(bits_converted, 1)
                act.wait_ge(bits_converted, c + 1)
                act.wait_ge(keys_turned, c - 1 + FREE)
                nc.scalar.activation(key_diag[:, k % 2, :], ident_h[:, :], ACT.Copy,
                                     scale=key_octet[:, k % 2, 0:1]).then_inc(keys_spread, 1)

            def mask(c, k):
                act.wait_ge(picked, c + 1 + FREE)
                act.wait_ge(octets_marked, c + 1 + FREE)
                act.wait_ge(chosen, c + FREE)
                for o in range(OCTET):
                    last = nc.scalar.activation(masked[:, o, :], ps_g[:, k % 2, o * C:(o + 1) * C], ACT.Copy,
                                                scale=octet_is[:, k % RING, o:o + 1])
                last.then_inc(octet_masked, 1)

            def copy_keys(c, k):
                act.wait_ge(keys_turned, c + 1 + FREE)
                act.wait_ge(keys_matched, c - 1 + FREE)
                nc.scalar.activation(key_row[:, k % 2, :], ps_k, ACT.Copy).then_inc(keys_ready, 1)

            def step(c, k, tiles=CHUNK):
                if tiles == CHUNK:
                    flags(c + 1, k + 1)
                    spread_keys(c + KEYS_AHEAD, k + KEYS_AHEAD)
                for g, n in groups(tiles):
                    act.wait_ge(z_turned, c * GROUPS + g + 1)
                    full = n // 2 * P
                    last = nc.scalar.activation(zt[:, g, 0:full], ps_t[:, g, 0:full], ACT.Relu)
                    if n % 2:
                        last = nc.scalar.activation(zt[0:C, g, full:full + P], ps_t[0:C, g, full:full + P], ACT.Relu)
                    last.then_inc(relu_done, 1)
                if tiles == CHUNK:
                    mask(c + CHOOSE_AHEAD, k + CHOOSE_AHEAD)
                    copy_keys(c + KEYS_AHEAD, k + KEYS_AHEAD)
                act.wait_ge(max_step, c * CHUNK + tiles + 1)
                act.dma_start(state_lanes[:, bass.ds(c * W, tiles * C)], state[:, k % 2, 0:tiles * C]
                              ).then_inc(state_stored[k % 2], 16)

            for g in range(PAGES):
                page_loads = g // 2 + 1
                if g == PAGES - 1:
                    page_loads += PARTS * (1 + (N % OCTET > 0)) - 1
                act.wait_ge(page_loaded[g % 2], 16 * page_loads)
                if g == 0:
                    act.wait_ge(b_stored, 16 * PIECES)
                for t in range(PARTS):
                    if t >= 1:
                        act.wait_ge(page_left, 1 + g * (PARTS - 1) + t)
                    nc.scalar.activation(table[:, g, t, :], page[:, g % 2, :], ACT.Copy).then_inc(page_part, 1)
            act.wait_ge(page_part, PAGES * PARTS)
            for t in range(1, PARTS):
                quarter = slice(t * QUARTER, (t + 1) * QUARTER)
                nc.scalar.activation(table[quarter, PAGES - 1, 0, :], table[quarter, PAGES - 1, t, :],
                                     ACT.Copy).then_inc(table_ready, 1)

            act.wait_ge(same_ready, 1)
            flags(0, 0)
            for half in range(2):
                act.sem_inc(state_stored[half], 16)
            act.sem_inc(keys_ready, 1)
            act.sem_inc(octet_masked, FREE)
            act.sem_inc(keys_spread, FREE)
            for c in range(-KEYS_AHEAD, 0):
                spread_keys(c + KEYS_AHEAD, c + KEYS_AHEAD)
                copy_keys(c + KEYS_AHEAD, c + KEYS_AHEAD)
            mask(0, 0)
            act.wait_ge(a_scattered, 16 * NJ)
            nc.scalar.activation(a_rows[0:NP, :, :], b2_rows[0:NP, :].rearrange("p (o c) -> p o c", o=1)
                                 .to_broadcast((NP, NJ, C)), ACT.Copy, scale=-1.0).then_inc(maxima_preset, 1)
            with act.Fori(0, ITERS) as i:
                for k in range(RING):
                    step(i * RING + k, k)
            step(CHUNKS, 0, TAIL)
            act.wait_ge(state_stored[0], 16 * (CHUNKS // 2 + 2))
            act.wait_ge(state_stored[1], 16 * (CHUNKS // 2 + 1))

        @block.tensor
        def _(pe):
            pe.wait_ge(samples_marked, 1)
            for m in range(SCOLS):
                nc.tensor.matmul(ps_s[0:NP, 0:SEARCHES], above[0:NP, m, 0:NP], ones_b[0:NP, :], start=m == 0, stop=False)
                last = nc.tensor.matmul(ps_s[0:NP, 0:SEARCHES], inside[0:NP, m, 0:NP], column[0:NP, m, :],
                                        start=False, stop=m == SCOLS - 1)
            last.then_inc(samples_counted, 1)
            pe.wait_ge(pool_const, 3)

            def turn_h(g):
                if 4 * g % PJ == 0:
                    pe.wait_ge(h_ready, 4 * g // PJ + 1)
                if g >= 2:
                    pe.wait_ge(ht_ready, g - 1)
                for a in range(2):
                    last = nc.tensor.transpose(ps_t[:, g % 2, a * NP:(a + 1) * NP],
                                               xs[0:NP, 4 * g + 2 * a:4 * g + 2 * a + 2, :].rearrange("p j c -> p (j c)"),
                                               ident[0:NP, 0:NP])
                last.then_inc(ht_ps, 1)

            def products(g):
                pe.wait_ge(ht_ready, g + 1)
                if g >= 2:
                    pe.wait_ge(a_ready, g - 1)
                    pe.wait_ge(b_ready, g - 1)
                for a in range(2):
                    last = nc.tensor.matmul(ps_m[0:NP, g % 2, a * 2 * P:(a + 1) * 2 * P], ht[:, g % 2, a * NP:(a + 1) * NP],
                                            w1_diag[:, :, :, :].rearrange("p h w n -> p (h w n)"), start=True, stop=True)
                last.then_inc(ab_ps, 1)

            pe.wait_ge(w1_ready, 4)
            for g in range(NJ // 4 + 1):
                if g < NJ // 4:
                    turn_h(g)
                if g >= 1:
                    products(g - 1)

            pe.wait_ge(blk_ready, 1)
            pe.wait_ge(diag_ready, 1)
            for f in range(2):
                last = nc.tensor.matmul(ps_s[0:C, f * P:(f + 1) * P], ones[:, 0:C], diag[:, f, :], start=True, stop=True)
            last.then_inc(caps_ps, 1)
            pe.wait_ge(w2_loaded, 32)
            pe.wait_ge(a_ready, NJ // 4)
            pe.wait_ge(b_ready, NJ // 4)

            w2_pair = w2_diag[:, :, :].rearrange("p h n -> p (h n)")

            def turn_keys(c, k):
                pe.wait_ge(keys_spread, c + 1 + FREE)
                pe.wait_ge(keys_ready, c + 1)
                nc.tensor.matmul(ps_k, ones_h[:, :], key_diag[:, k % 2, :], start=True, stop=True).then_inc(keys_turned, 1)

            def pick(c, k, pages):
                half = k % 2
                if pages[0] == 0:
                    pe.wait_ge(keys_matched, c + 1 + FREE)
                    pe.wait_ge(octet_masked, c - 1 + FREE)
                for g in pages:
                    for t in range(PARTS if g < PAGES - 1 else 1):
                        last = nc.tensor.matmul(ps_g[:, half, :], key_is[:, half, g, :], table[:, g, t, :],
                                                start=(g, t) == (0, 0), stop=g == PAGES - 1)
                if pages[-1] == PAGES - 1:
                    last.then_inc(picked, 1)

            def step(c, k, tiles=CHUNK):
                whole = tiles == CHUNK
                for g, n in groups(tiles):
                    pe.wait_ge(z_ready, c * GROUPS + g + 1)
                    for a, m in pairs(n):
                        t = g * GROUP + a
                        last = nc.tensor.transpose(ps_t[0:m * C, g, a * C:a * C + P],
                                                   rows[:, k, t * C:(t + m) * C], ident[:, :])
                    last.then_inc(z_turned, 1)
                if whole:
                    pick(c + PICK_AHEAD, k + PICK_AHEAD, range(0, 1))
                for g, n in groups(tiles):
                    pe.wait_ge(relu_done, c * GROUPS + g + 1)
                    for a, m in pairs(n):
                        last = nc.tensor.matmul(ps_m[:, g, a * C:(a + m) * C], zt[0:m * C, g, a * C:a * C + P],
                                                w2_pair[0:m * C, 0:m * C], start=True, stop=True)
                    last.then_inc(messages, 1)
                if whole:
                    turn_keys(c + KEYS_AHEAD, k + KEYS_AHEAD)
                    pick(c + PICK_AHEAD, k + PICK_AHEAD, range(1, PAGES))

            pe.sem_inc(picked, FREE)
            pe.sem_inc(keys_turned, FREE)
            pe.wait_ge(table_ready, PARTS - 1)
            pe.wait_ge(caps_ready, 1)
            for c in range(-KEYS_AHEAD, 0):
                turn_keys(c + KEYS_AHEAD, c + KEYS_AHEAD)
                if c >= -PICK_AHEAD:
                    pick(c + PICK_AHEAD, c + PICK_AHEAD, range(PAGES))
            with pe.Fori(0, ITERS) as i:
                for k in range(RING):
                    step(i * RING + k, k)
            step(CHUNKS, 0, TAIL)

            pe.wait_ge(max_step, CHUNKS * CHUNK + TAIL + 1)
            nc.tensor.transpose(ps_s[0:C, P:2 * P], state[:, 0, (TAIL - 1) * C:TAIL * C], ident[:, :]).then_inc(last_turned, 1)
            pe.wait_ge(carry_ready, 1)
            nc.tensor.transpose(ps_s[:, 2 * P:2 * P + C], carry_cap[:, :], ident[0:C, 0:C]).then_inc(carry_turned, 1)

        @block.vector
        def _(dve):
            steps = [0]

            def link(instruction):
                steps[0] += 1
                instruction.then_inc(dve_step, 1)
                dve.wait_ge(dve_step, steps[0])

            nc.vector.memset(w2_diag[:, :, :], 0.0).then_inc(w2_cleared, 1)
            nc.vector.memset(state[:, :, :], 0.0).then_inc(zero_row_set, 1)
            nc.vector.memset(eps[:, :], EPS)
            nc.vector.memset(page[:, :, :], 0.0).then_inc(page_left, 1)
            link(nc.vector.memset(w1_diag[:, :, :, :], 0.0))
            nc.vector.memset(ones_b[:, :], 1.0)
            nc.vector.memset(same[:, TILES:], 0.0)
            nc.vector.memset(dst_all[0:1, 0:1], -1)
            nc.vector.memset(ones_h[:, :], 1.0)
            dve.wait_ge(pool_ranks, 2)
            link(nc.vector.tensor_copy(rank[:, :], rank_i[:, :]))
            link(nc.vector.tensor_scalar(base[:, :], rank[:, 0:P], float(NJ), None, ALU.mult))
            dve.wait_ge(samples_loaded, 16)
            link(nc.vector.tensor_copy(smp[0:NP, 0, :], smp_i[0:NP, :]))
            for m in range(SCOLS):
                last = nc.vector.tensor_scalar(above[0:NP, m, 0:NP], base[0:NP, 0:NP], smp[0:NP, 0, m:m + 1], None, ALU.is_gt)
            link(last)
            link(nc.vector.tensor_reduce(smp[0:NP, 1, :], above[0:NP, :, 0:NP], AX_X, ALU.add))
            link(nc.vector.tensor_scalar(smp[0:NP, 2, :], smp[0:NP, 1, :], -1.0, float(NP - 1), ALU.mult, ALU.add))
            link(nc.vector.scalar_tensor_tensor(smp[0:NP, 3, :], smp[0:NP, 2, :], -float(NJ), smp[0:NP, 0, :],
                                                ALU.mult, ALU.add))
            for m in range(SCOLS):
                nc.vector.tensor_scalar(inside[0:NP, m, 0:NP], rank[0:NP, 0:NP], smp[0:NP, 2, m:m + 1], None, ALU.is_equal)
                last = nc.vector.tensor_scalar(column[0:NP, m, :], rank[0:NP, 0:SEARCHES], smp[0:NP, 3, m:m + 1], None,
                                               ALU.is_gt)
            last.then_inc(samples_marked, 1)
            dve.wait_ge(pool_const, 3)
            nc.vector.tensor_scalar(nid_half[0:NP, :], nid_i[0:NP, :], -0.5, None, ALU.add).then_inc(consts_set, 1)
            dve.wait_ge(samples_counted, 1)
            link(nc.vector.tensor_scalar(blk[0:NP, :], ps_s[0:NP, 0:SEARCHES], -1.0, 0.0, ALU.add, ALU.max))
            nc.vector.tensor_copy(blk_idx[0:NP, :], blk[0:NP, :]).then_inc(blk_ready, 1)
            dve.wait_ge(weights_loaded, 64)
            for h in range(2):
                half = slice(h * C, (h + 1) * C)
                nc.vector.tensor_tensor(w1_diag[half, h, 0, :], w1_raw[half, 0, :], w1_raw[half, 1, :],
                                        ALU.subtract).then_inc(w1_ready, 1)
                nc.vector.tensor_copy(w1_diag[half, h, 1, :], w1_raw[half, 1, :]).then_inc(w1_ready, 1)

            def piece(q):
                return xs[0:NP, q * PJ:(q + 1) * PJ, :]

            def spread(values):
                return values.rearrange("p (j o) -> p j o", o=1).to_broadcast((NP, PJ, C))

            def centre(q):
                dve.wait_ge(x_loaded[q], 16)
                s = stat[0:NP, q, :, :]
                link(nc.vector.tensor_reduce(s[:, 0, :], piece(q), AX_X, ALU.add))
                link(nc.vector.tensor_scalar(s[:, 1, :], s[:, 0, :], 1.0 / C, None, ALU.mult))
                nc.vector.tensor_tensor(piece(q), piece(q), spread(s[:, 1, :]), ALU.subtract).then_inc(centred, 1)

            def scale(q):
                s = stat[0:NP, q, :, :]
                dve.wait_ge(squared, q + 1)
                nc.vector.tensor_reduce(s[:, 2, :], squares[0:NP, :].rearrange("p (j c) -> p j c", c=C),
                                        AX_X, ALU.add).then_inc(var_ready, 1)
                dve.wait_ge(sd_ready, q + 1)
                link(nc.vector.reciprocal(s[:, 4, :], s[:, 3, :]))
                nc.vector.tensor_tensor(piece(q), piece(q), spread(s[:, 4, :]), ALU.mult).then_inc(h_ready, 1)

            for q in range(PIECES + 1):
                if q < PIECES:
                    centre(q)
                if q >= 1:
                    scale(q - 1)

            def lanes():
                dve.wait_ge(dst_loaded, 32)
                nc.vector.tensor_scalar(lane[:, 0:1], dst_all[:, 1:2], 0.5, None, ALU.add).then_inc(lane_idx_ready, 1)
                link(nc.vector.tensor_tensor(same[:, 0:TILES], dst_all[:, 1:], dst_all[:, 0:TILES], ALU.is_equal))
                link(nc.vector.tensor_tensor(lane[:, 2:3], dst_all[:, 1:2], dst_all[:, TILES:TILES + 1], ALU.is_equal))
                link(nc.vector.tensor_tensor(lane[:, 3:4], lane[:, 2:3], same[:, 0:1], ALU.mult))
                dve.wait_ge(pool_const, 3)
                nc.vector.tensor_scalar(diag[:, 0, :], ident[:, :], same[:, 0:1], None, ALU.mult)
                nc.vector.tensor_scalar(diag[:, 1, :], ident[:, :], lane[:, 3:4], None, ALU.mult).then_inc(diag_ready, 1)
                dve.wait_ge(diag_ready, 1)
                nc.vector.tensor_scalar(same[:, 0:TILES], same[:, 0:TILES], 2.0, -1.0, ALU.mult, ALU.add).then_inc(same_ready, 1)
                dve.wait_ge(caps_ps, 1)
                link(nc.vector.tensor_scalar(caps[:, :, :].rearrange("p f q -> p (f q)"), ps_s[0:C, 0:2 * P],
                                             2.0, -1.0, ALU.mult, ALU.add))
                link(nc.vector.tensor_scalar(caps[:, :, :], caps[:, :, :], FLT_MAX, None, ALU.mult))

            for g in range(NJ // 4):
                dve.wait_ge(ab_ps, g + 1)
                nc.vector.tensor_tensor(a_rows[0:NP, 4 * g:4 * g + 4, :],
                                        ps_m[0:NP, g % 2, :].rearrange("p (j w) -> p j w", j=4)[:, :, 0:C],
                                        b1_rows[0:NP, :].rearrange("p (o c) -> p o c", o=1).to_broadcast((NP, 4, C)),
                                        ALU.add).then_inc(a_ready, 1)
            lanes()
            dve.wait_ge(blk_used, SEARCHES)
            link(nc.vector.tensor_scalar(below[0:NP, :], below[0:NP, :], 0.5, BLOCK / 2.0, ALU.mult, ALU.add))
            link(nc.vector.scalar_tensor_tensor(first[0:NP, :], blk[0:NP, :], float(BLOCK), below[0:NP, :], ALU.mult, ALU.add))
            link(nc.vector.tensor_tensor(empty[0:NP, :], first[0:NP, 0:NJ], first[0:NP, 1:SEARCHES], ALU.is_equal))
            nc.vector.scalar_tensor_tensor(first_idx[0:NP, :], empty[0:NP, :], OUT_OF_RANGE, first[0:NP, 0:NJ],
                                           ALU.mult, ALU.add).then_inc(scatter_ready, 1)
            link(nc.vector.tensor_scalar(tmp_n[0:NP, :], first[0:NP, 1:SEARCHES], -1.0, 0.0, ALU.add, ALU.max))
            nc.vector.scalar_tensor_tensor(last_idx[0:NP, :], empty[0:NP, :], OUT_OF_RANGE, tmp_n[0:NP, :],
                                           ALU.mult, ALU.add)

            dve.wait_ge(first_count, 1)
            link(nc.vector.tensor_scalar(lane[:, 4:5], lane[:, 1:2], float(TILES), 0.5, ALU.add, ALU.mult))
            link(nc.vector.tensor_copy(lane[:, 5:6], lane_i[:, 0:1]))
            nc.vector.tensor_tensor(lane_i[:, 1:2], lane[:, 4:5], lane[:, 5:6], ALU.add).then_inc(caps_ready, 1)

            nc.vector.tensor_copy(ident_h[:, :], ident[:, :])
            link(nc.vector.tensor_copy(page_keys[:, :], page_i[:, :]))
            for t in range(1, PARTS):
                quarter = page_keys[t * QUARTER:(t + 1) * QUARTER, PAGES - 1:PAGES]
                nc.vector.tensor_scalar(quarter, quarter, -float(t * QUARTER), None, ALU.add)
            nc.vector.tensor_copy(octets[:, :], rank[:, 0:OCTET]).then_inc(picks_set, 1)
            for g in range(PAGES):
                for t in range(PARTS - 1):
                    dve.wait_ge(page_part, g * PARTS + t + 1)
                    nc.vector.tensor_tensor(page[:, g % 2, :], page[:, g % 2, :], table[:, g, t, :],
                                            ALU.subtract).then_inc(page_left, 1)

            for half in range(2):
                dve.wait_ge(zeros_stored[half], 16 * ZEROS // 2)
            nc.vector.memset(state[:, 1, W - C:W], -FLT_MAX).then_inc(a_free, AE_RING - 1)
            dve.wait_ge(fill_init, 16)
            dve.wait_ge(a_free, AE_RING - 1)
            dve.wait_ge(picks_set, 1)
            dve.sem_inc(max_step, 1)
            dve.sem_inc(octets_marked, FREE)
            dve.sem_inc(keys_matched, FREE)
            dve.sem_inc(chosen, FREE)
            dve.wait_ge(src_first, 16)

            def fill_ready(c, k, i):
                slot = k % AE_RING
                dve.wait_ge(a_loaded[slot], (i * (RING // AE_RING) + k // AE_RING + 1) * 16)
                dve.wait_ge(keep_ready, c + 1)

            def fill(c, k, t):
                slot = k % AE_RING
                if t == 0:
                    before = a_fill[:, (slot - 1) % AE_RING, W - C:W]
                else:
                    before = a_fill[:, slot, (t - 1) * C:t * C]
                    dve.wait_ge(fill_step, c * CHUNK + t)
                if t == 1:
                    dve.sem_inc(a_free, 1)
                here = a_fill[:, slot, t * C:(t + 1) * C]
                nc.vector.scalar_tensor_tensor(here, before, keep[:, k % KEEP, 0, t:t + 1], here,
                                               ALU.mult, ALU.add).then_inc(fill_step, 1)

            def add(c, k, i, tiles=CHUNK):
                dve.wait_ge(fill_step, (c + 1) * CHUNK)
                if tiles == CHUNK:
                    dve.wait_ge(gathered[k], (i + 1) * 16 * GATHERED)
                    dve.wait_ge(chosen, c + 1 + FREE)
                else:
                    dve.wait_ge(gathered[k], (ITERS * GATHERED + tiles) * 16)
                for g, n in groups(tiles):
                    part = slice(g * GROUP * C, (g * GROUP + n) * C)
                    nc.vector.tensor_tensor(rows[:, k, part], rows[:, k, part], a_fill[:, k % AE_RING, part],
                                            ALU.add).then_inc(z_ready, 1)

            def maximum(c, k, t):
                half = k % 2
                g, r = divmod(t, GROUP)
                if r == 0:
                    dve.wait_ge(messages, c * GROUPS + g + 1)
                if t == 0:
                    before = state[:, 1 - half, W - C:W]
                else:
                    before = state[:, half, (t - 1) * C:t * C]
                dve.wait_ge(max_step, c * CHUNK + t + 1)
                nc.vector.scalar_tensor_tensor(state[:, half, t * C:(t + 1) * C], before,
                                               keep[:, k % KEEP, 1, t:t + 1], ps_m[:, g, r * C:(r + 1) * C],
                                               ALU.min, ALU.max).then_inc(max_step, 1)

            def split_src(c, k, i):
                column = src_idx[:, k, CHUNK - 1:CHUNK]
                dve.wait_ge(src_loaded[k // 2], (i + 1) * 32)
                dve.wait_ge(keys_spread, c - 1 + FREE)
                nc.vector.tensor_scalar(key_bits[:, k % 2, 0:1], column, 3, None, ALU.logical_shift_right)
                nc.vector.tensor_scalar(key_bits[:, k % 2, 1:2], column, OCTET - 1, None,
                                        ALU.bitwise_and).then_inc(bits_split, 1)

            def mark_octets(c, k):
                dve.wait_ge(bits_converted, c + 1)
                nc.vector.tensor_scalar(octet_is[:, k, :], octets[:, :], key_octet[:, k % 2, 1:2], None,
                                        ALU.is_equal).then_inc(octets_marked, 1)

            def match_keys(c, k):
                half = k % 2
                dve.wait_ge(keys_ready, c + 1 + 1)
                dve.wait_ge(picked, c - 1 + FREE)
                nc.vector.tensor_tensor(
                    key_is[:, half, :, :],
                    key_row[:, half, :].rearrange("p (o e) -> p o e", o=1).to_broadcast((P, PAGES, P)),
                    page_keys[:, :].rearrange("p (g o) -> p g o", o=1).to_broadcast((P, PAGES, P)),
                    ALU.is_equal).then_inc(keys_matched, 1)

            def choose(c, k):
                dve.wait_ge(octet_masked, c + 1 + FREE)
                nc.vector.tensor_reduce(rows[:, k, W - C:W], masked[:, :, :].rearrange("p o c -> p c o"),
                                        AX_X, ALU.add).then_inc(chosen, 1)

            def prepare_picks(c, k, i, match=True):
                def ahead(chunks):
                    return c + chunks, (k + chunks) % RING

                split_src(*ahead(KEYS_AHEAD), i + (k + KEYS_AHEAD) // RING)
                if match:
                    match_keys(*ahead(MATCH_AHEAD))
                mark_octets(*ahead(KEYS_AHEAD))

            for c in range(-KEYS_AHEAD, 0):
                prepare_picks(c, c, 0, match=c >= -MATCH_AHEAD)
            choose(0, 0)

            LEAD = 2
            fill_ready(0, 0, 0)
            for t in range(CHUNK):
                fill(0, 0, t)
            with dve.Fori(0, ITERS) as i:
                for k in range(RING):
                    c = i * RING + k
                    add(c, k, i)
                    prepare_picks(c, k, i)
                    fill_ready(c + 1, (k + 1) % RING, i + (k + 1) // RING)
                    dve.wait_ge(state_stored[k % 2], (i * (RING // 2) + k // 2 + 1) * 16)
                    for t in range(CHUNK + LEAD):
                        if t == CHUNK - 2:
                            choose(c + CHOOSE_AHEAD, (k + CHOOSE_AHEAD) % RING)
                        if t < CHUNK:
                            fill(c + 1, (k + 1) % RING, t)
                        if t >= LEAD:
                            maximum(c, k, t - LEAD)
            add(CHUNKS, 0, ITERS, TAIL)
            dve.wait_ge(state_stored[0], (ITERS * (RING // 2) + 1) * 16)
            for t in range(TAIL):
                maximum(CHUNKS, 0, t)

            dve.wait_ge(last_turned, 1)
            nc.vector.memset(carry[:, 0:1], -FLT_MAX)
            link(nc.vector.tensor_tensor_scan(carry[:, 1:P], caps[:, 1, 0:P - 1], ps_s[0:C, P:2 * P - 1], -FLT_MAX,
                                              ALU.min, ALU.max))
            nc.vector.tensor_tensor(carry_cap[:, :], carry[:, :], caps[:, 0, :], ALU.min).then_inc(carry_ready, 1)
            dve.wait_ge(carry_turned, 1)
            dve.wait_ge(head_loaded, 16)
            nc.vector.tensor_tensor(head_new[:, :], head[:, :], ps_s[:, 2 * P:2 * P + C], ALU.max).then_inc(head_ready, 1)

            dve.wait_ge(x_again, 16)
            for g in range(NJ // BATCH):
                dve.wait_ge(maxima[g], 16 * BATCH)
                part = a_rows[0:NP, g * BATCH:(g + 1) * BATCH, :]
                link(nc.vector.tensor_tensor(part, part, b2_rows[0:NP, :].rearrange("p (o c) -> p o c", o=1)
                                             .to_broadcast((NP, BATCH, C)), ALU.add))
                nc.vector.tensor_tensor(part, part, xs[0:NP, g * BATCH:(g + 1) * BATCH, :], ALU.add).then_inc(out_ready, 1)


_INS = ["x", "src", "dst", "L0_gnn_W1", "L0_gnn_b1", "L0_gnn_W2", "L0_gnn_b2"]


def kernel(**inputs):
    import numpy as _np
    import concourse.bacc as _bacc
    from concourse import mybir as _mybir
    from concourse.bass_utils import run_bass_kernel_spmd as _run

    nc = _bacc.Bacc("TRN2", target_bir_lowering=False, num_devices=1)
    arrays, args = {}, []
    for name in _INS:
        a = _np.ascontiguousarray(inputs[name])
        arrays[f"in_{name}_dram"] = a
        args.append(nc.dram_tensor(f"in_{name}_dram", a.shape, _mybir.dt.from_np(a.dtype), kind="ExternalInput").ap())
    shape = arrays["in_x_dram"].shape
    args.append(nc.dram_tensor("out_dram", shape, _mybir.dt.float32, kind="ExternalOutput").ap())
    edge_conv(nc, *args)
    r = _run(nc, [arrays], core_ids=[0])
    return r.results[0]["out_dram"]
```
